# Optimizing a Trainium2 kernel written in Bass

```python
import numpy as np
import jax
import jax.numpy as jnp

def _softmax(x, axis=-1):
    return jax.nn.softmax(x, axis=axis)

def _gelu(x):
    return jax.nn.gelu(x, approximate=True)

def _silu(x):
    return jax.nn.silu(x)

def _sigmoid(x):
    return jax.nn.sigmoid(x)

def _layernorm(x, axis=-1, eps=1e-05):
    m = jnp.mean(x, axis=axis, keepdims=True)
    v = jnp.var(x, axis=axis, keepdims=True)
    return (x - m) / jnp.sqrt(v + eps)

def _scatter_add(tgt, idx, src, axis=0):
    return tgt.at[idx].add(src)

def _segment_sum(src, seg, n):
    return jax.ops.segment_sum(src, seg, n)
kernel_name = 'mk_seq_postln_d1_jaxref_r8_9f6494'

def setup_inputs(seed: int=0):
    np.random.seed(seed)
    _w = jnp.asarray

    def _L0_attn_setup():
        import jax, jax.numpy as jnp
        import numpy as np
        import math
        DIM = 128
        NUM_HEADS = 16
        HEAD_DIM = DIM // NUM_HEADS
        BATCH = 4
        SEQ = 512

        def _feature_map(x, R):
            x = x / math.sqrt(HEAD_DIM)
            proj = jnp.einsum('bhnd,dm->bhnm', x, R)
            sq_norm = jnp.sum(x * x, axis=-1, keepdims=True)
            return jnp.exp(proj - 0.5 * sq_norm)
        key = jax.random.key(seed)
        ks = jax.random.split(key, 10)
        s = 1.0 / math.sqrt(DIM)
        return {'x': jax.random.normal(ks[0], (BATCH, SEQ, DIM), dtype=jnp.float32), 'Wq': jax.random.normal(ks[1], (DIM, DIM), dtype=jnp.float32) * s, 'bq': jax.random.normal(ks[2], (DIM,), dtype=jnp.float32) * 0.01, 'Wk': jax.random.normal(ks[3], (DIM, DIM), dtype=jnp.float32) * s, 'bk': jax.random.normal(ks[4], (DIM,), dtype=jnp.float32) * 0.01, 'Wv': jax.random.normal(ks[5], (DIM, DIM), dtype=jnp.float32) * s, 'bv': jax.random.normal(ks[6], (DIM,), dtype=jnp.float32) * 0.01, 'Wo': jax.random.normal(ks[7], (DIM, DIM), dtype=jnp.float32) * s, 'bo': jax.random.normal(ks[8], (DIM,), dtype=jnp.float32) * 0.01, 'R': jax.random.normal(ks[9], (HEAD_DIM, HEAD_DIM), dtype=jnp.float32) * 0.4}
    _L0_attn_in = _L0_attn_setup()

    def _L0_ffn_setup():
        import jax, jax.numpy as jnp
        import numpy as np
        E, H, I, K = (8, 128, 256, 2)
        B, S = (4, 256)
        key = jax.random.key(seed)
        k1, k2, k3, k4 = jax.random.split(key, 4)
        x = jax.random.normal(k1, (B, S, H), dtype=jnp.float32)
        router_w = jax.random.uniform(k2, (E, H), dtype=jnp.float32, minval=-1.0, maxval=1.0) / np.sqrt(H).astype(np.float32)
        w13 = jax.random.normal(k3, (E, H, 2 * I), dtype=jnp.float32) * 0.02
        w2 = jax.random.normal(k4, (E, I, H), dtype=jnp.float32) * 0.02
        return {'x': x, 'router_w': router_w, 'w13': w13, 'w2': w2}
    _L0_ffn_in = _L0_ffn_setup()
    _d = {'L0_attn_x': _L0_attn_in['x'], 'L0_attn_Wq': _L0_attn_in['Wq'], 'L0_attn_bq': _L0_attn_in['bq'], 'L0_attn_Wk': _L0_attn_in['Wk'], 'L0_attn_bk': _L0_attn_in['bk'], 'L0_attn_Wv': _L0_attn_in['Wv'], 'L0_attn_bv': _L0_attn_in['bv'], 'L0_attn_Wo': _L0_attn_in['Wo'], 'L0_attn_bo': _L0_attn_in['bo'], 'L0_attn_R': _L0_attn_in['R'], 'L0_ffn_router_w': _L0_ffn_in['router_w'], 'L0_ffn_w13': _L0_ffn_in['w13'], 'L0_ffn_w2': _L0_ffn_in['w2']}
    _x0 = _d['L0_attn_x']
    _d['L0_attn_x'] = jax.random.normal(jax.random.fold_in(jax.random.key(seed), 1), (32, 256, 128), dtype=_x0.dtype)
    del _x0
    return _d

def reference(L0_attn_x, L0_attn_Wq, L0_attn_bq, L0_attn_Wk, L0_attn_bk, L0_attn_Wv, L0_attn_bv, L0_attn_Wo, L0_attn_bo, L0_attn_R, L0_ffn_router_w, L0_ffn_w13, L0_ffn_w2):

    def _L0_attn_ref(x, Wq, bq, Wk, bk, Wv, bv, Wo, bo, R):
        import jax, jax.numpy as jnp
        import numpy as np
        import math
        DIM = 128
        NUM_HEADS = 16
        HEAD_DIM = DIM // NUM_HEADS
        BATCH = 4
        SEQ = 512

        def _feature_map(x, R):
            x = x / math.sqrt(HEAD_DIM)
            proj = jnp.einsum('bhnd,dm->bhnm', x, R)
            sq_norm = jnp.sum(x * x, axis=-1, keepdims=True)
            return jnp.exp(proj - 0.5 * sq_norm)
        b, n, _ = x.shape
        h, d = (NUM_HEADS, HEAD_DIM)

        def split_heads(t):
            return t.reshape(b, n, h, d).transpose(0, 2, 1, 3)
        q = split_heads(x @ Wq.T + bq)
        k = split_heads(x @ Wk.T + bk)
        v = split_heads(x @ Wv.T + bv)
        q_prime = _feature_map(q, R)
        k_prime = _feature_map(k, R)
        kv = jnp.einsum('bhnd,bhne->bhde', k_prime, v)
        z = 1.0 / (jnp.sum(q_prime, axis=-1) + 1e-08)
        out = jnp.einsum('bhnd,bhde,bhn->bhne', q_prime, kv, z)
        out = out.transpose(0, 2, 1, 3).reshape(b, n, DIM)
        return out @ Wo.T + bo

    def _L0_ffn_ref(x, router_w, w13, w2):
        import jax, jax.numpy as jnp
        import numpy as np
        E, H, I, K = (8, 128, 256, 2)
        B, S = (4, 256)
        logits = jnp.einsum('bsh,eh->bse', x, router_w)
        probs = jax.nn.softmax(logits, axis=-1)
        weights, indices = jax.lax.top_k(probs, K)
        weights = weights / (weights.sum(axis=-1, keepdims=True) + 1e-06)
        h13 = jnp.einsum('bsh,ehi->bsei', x, w13)
        gate, up = jnp.split(h13, 2, axis=-1)
        h = jax.nn.silu(gate) * up
        y = jnp.einsum('bsei,eih->bseh', h, w2)
        y_sel = jnp.take_along_axis(y, indices[..., None], axis=2)
        return (y_sel * weights[..., None]).sum(axis=2)
    x = L0_attn_x
    x = _layernorm(x + _L0_attn_ref(x, L0_attn_Wq, L0_attn_bq, L0_attn_Wk, L0_attn_bk, L0_attn_Wv, L0_attn_bv, L0_attn_Wo, L0_attn_bo, L0_attn_R), axis=-1)
    x = _layernorm(x + _L0_ffn_ref(x, L0_ffn_router_w, L0_ffn_w13, L0_ffn_w2), axis=-1)
    return x

_drawn_inputs = setup_inputs


def setup_inputs(seed=0):
    import zlib

    import numpy as np

    out = dict(_drawn_inputs(seed))
    spreads = {}
    factors = {'L0_attn_bq': 8.0,
     'L0_attn_bk': 8.0,
     'L0_attn_bo': 8.0,
     'L0_ffn_router_w': 8.0,
     'L0_ffn_w13': 8.0,
     'L0_ffn_w2': 8.0}
    for name, (base, spread) in spreads.items():
        noise = np.random.default_rng([zlib.crc32(name.encode()), seed]).standard_normal(out[name].shape)
        drawn = base * np.exp(spread * noise) if base else spread * noise
        out[name] = jnp.asarray(drawn.astype(out[name].dtype))
    for name, factor in factors.items():
        out[name] = (out[name] * factor).astype(out[name].dtype)
    return out
```

```python
from contextlib import ExitStack

import numpy as np

import concourse.bass as bass
from concourse import mybir

ALU = mybir.AluOpType
ACT = mybir.ActivationFunctionType
F32 = mybir.dt.float32
BF16 = mybir.dt.bfloat16
U32 = mybir.dt.uint32
I32 = mybir.dt.int32
AX_X = mybir.AxisListType.X

P = 128
DIM = 128
HEADS = 16
HEAD_DIM = DIM // HEADS
BATCHES, SEQ = 32, 256
TOKENS = BATCHES * SEQ
EXPERTS = 8
INNER = 256
TOP_K = 2
LN_EPS = 1e-5

GT = 4
GROUPS = TOKENS // (GT * P)
TILES = TOKENS // P
HALVES = 2
HALF_GROUPS = GROUPS // HALVES
PAYLOAD = 4
ROW = DIM + PAYLOAD
CHOICES = TOP_K * TOKENS
HALF_CHOICES = CHOICES // HALVES
UNROLL = 8
BLOCKS = -(-(HALF_CHOICES // P + EXPERTS - 1) // UNROLL) * UNROLL
REGION = TOKENS // HALVES + P
HALF_ROWS = EXPERTS * REGION + UNROLL * P
FILLS = HALVES * (EXPERTS + UNROLL)
TURNS = HALVES * BLOCKS // UNROLL


def moe_kernel(nc, x, wqT, wq, bq, wkT, wk, bk, wvT, bv_rows, woT, bo_rows, r_tiled,
               router_wT, w13, w2, out):
    with ExitStack() as ctx:
        def sb(name, shape, dt=F32):
            return ctx.enter_context(nc.sbuf_tensor(name, shape, dt))

        def bank(name, shape, dt=F32):
            return ctx.enter_context(nc.psum_tensor(name, shape, dt))

        def sem(name):
            return ctx.enter_context(nc.semaphore(name))

        sorted_rows = nc.dram_tensor("sorted_rows", [HALVES * HALF_ROWS, ROW], F32, kind="Internal").ap()
        expert_out = nc.dram_tensor("expert_out", [CHOICES + FILLS * P, DIM], F32, kind="Internal").ap()

        wqT_s, wq_s, wkT_s, wk_s = (sb(n, [P, DIM]) for n in ("wqT_s", "wq_s", "wkT_s", "wk_s"))
        wvT_s, woT_s, bv_s, bo_s, r_s = (sb(n, [P, DIM]) for n in ("wvT_s", "woT_s", "bv_s", "bo_s", "r_s"))
        bq_s, bk_s = sb("bq_s", [P, 1]), sb("bk_s", [P, 1])
        router_s = sb("router_s", [P, EXPERTS])
        w13_s = sb("w13_s", [P, EXPERTS, 2 * INNER])
        w2_s = sb("w2_s", [P, EXPERTS, 2, DIM])
        ident = sb("ident", [P, P])
        head_mask = sb("head_mask", [P, HEADS, HEAD_DIM])
        neg_half_sum = sb("neg_half_sum", [P, P])
        blk_r = sb("blk_r", [P, P])
        wqrT, wkrT = sb("wqrT", [P, P]), sb("wkrT", [P, P])
        bqr, bkr = sb("bqr", [P, 1]), sb("bkr", [P, 1])
        before = sb("before", [P, P], BF16)
        ones_b = sb("ones_b", [P, P], BF16)
        bo_split = sb("bo_split", [P, GT, DIM], BF16)
        bo_rest = sb("bo_rest", [P, 2, DIM])
        iota_e = sb("iota_e", [P, EXPERTS], U32)
        iota_ei = sb("iota_ei", [P, EXPERTS], I32)
        minus_half = sb("minus_half", [P, GT])
        tok2_i = sb("tok2_i", [P, TILES], I32)
        fill_i = sb("fill_i", [P, FILLS], I32)
        fill_rows = sb("fill_rows", [P, FILLS, ROW])
        lane_i, lane_f = sb("lane_i", [P, 1], I32), sb("lane_f", [P, 1])
        region_i = sb("region_i", [P, HALVES, EXPERTS], I32)
        region_f = sb("region_f", [P, HALVES, EXPERTS])
        blk_i = sb("blk_i", [P, BLOCKS], I32)
        blk_f = sb("blk_f", [P, BLOCKS])
        blk_row_i = sb("blk_row_i", [P, HALVES, BLOCKS], I32)
        blk_row_f = sb("blk_row_f", [P, HALVES, BLOCKS])
        ones8 = sb("ones8", [P, EXPERTS])

        x_all = sb("x_all", [P, TILES, DIM])
        x_in = sb("x_in", [P, GT, DIM])
        xT = sb("xT", [P, GT * P])
        q_sq, k_sq = sb("q_sq", [P, GT * P]), sb("k_sq", [P, GT * P])
        q_feat, k_feat = sb("q_feat", [P, GT * P]), sb("k_feat", [P, GT * P])
        k_tok = sb("k_tok", [P, GT, DIM])
        v_tok = sb("v_tok", [P, GT, DIM])
        kv_den = sb("kv_den", [P, 2, DIM + HEADS])
        den = sb("den", [P, GT, HEADS])
        zrec = sb("zrec", [P, GT, HEADS])
        attn = sb("attn", [P, GT, DIM])
        attnT = sb("attnT", [P, GT, P])
        resid = sb("resid", [P, GT, DIM])
        stats = sb("stats", [P, GT, 6])
        meanvar = sb("meanvar", [P, GT, 2])
        var_eps = sb("var_eps", [P, GT])
        rstd = sb("rstd", [P, GT])
        x2T = sb("x2T", [P, GT, P])
        rows_now = sb("rows_now", [P, 2, GT, ROW])
        x2_all = sb("x2_all", [P, TILES, DIM])
        tok2_f = sb("tok2_f", [P, TILES])
        top8 = sb("top8", [P, GT, 8])
        idx8 = sb("idx8", [P, GT, 8], U32)
        gap8 = sb("gap8", [P, GT, 8])
        exp8 = sb("exp8", [P, GT, 8])
        sum8 = sb("sum8", [P, GT])
        wden = sb("wden", [P, GT])
        wden2 = sb("wden2", [P, GT])
        chosen = sb("chosen", [P, TOP_K, GT, EXPERTS], BF16)
        either = sb("either", [P, GT, EXPERTS], BF16)
        place = sb("place", [P, GROUPS + HALVES, GT + 1, EXPERTS])
        picked = sb("picked", [P, TOP_K, GT, EXPERTS])
        slots = sb("slots", [P, 2, GT, TOP_K], U32)

        fill_at_f = sb("fill_at_f", [P, EXPERTS])
        fill_at = sb("fill_at", [P, HALVES, EXPERTS], U32)
        count_f = sb("count_f", [P, EXPERTS])
        count_i = sb("count_i", [P, EXPERTS], I32)
        nblk_i = sb("nblk_i", [P, EXPERTS], I32)
        nblk_f = sb("nblk_f", [P, EXPERTS])
        end_f = sb("end_f", [P, EXPERTS])
        skip_f = sb("skip_f", [P, EXPERTS])
        past = sb("past", [P, BLOCKS, EXPERTS])
        past_skip = sb("past_skip", [P, BLOCKS, EXPERTS])
        blk_skip = sb("blk_skip", [P, BLOCKS])
        blk_expert = sb("blk_expert", [P, HALVES * BLOCKS])
        blk_expert_i = sb("blk_expert_i", [P, HALVES * BLOCKS], I32)
        blk_row = sb("blk_row", [P, HALVES * BLOCKS], I32)

        blk_in = sb("blk_in", [P, UNROLL, ROW])
        blk_xT = sb("blk_xT", [P, 2, P])
        silu_g = sb("silu_g", [P, 2, INNER])
        hidden = sb("hidden", [P, 2, INNER])
        hiddenT = sb("hiddenT", [P, 2, INNER])
        blk_out = sb("blk_out", [P, UNROLL, DIM])
        is_second = sb("is_second", [P, UNROLL])
        w_diff = sb("w_diff", [P, UNROLL])
        blk_w = sb("blk_w", [P, UNROLL])
        blk_dst = sb("blk_dst", [P, UNROLL], U32)

        pair_in = sb("pair_in", [P, 2, 2, TOP_K, 2 * DIM])
        fin = sb("fin", [P, 2, GT, DIM])

        B = [bank(f"bank{n}", [P, 512]) for n in range(8)]

        wts_in, xg_in, out_sem = sem("wts_in"), sem("xg_in"), sem("out_sem")
        ffn_in = sem("ffn_in")
        x_in_a, x_in_b = sem("x_in_a"), sem("x_in_b")
        dummy_out = sem("dummy_out")
        scattered = [sem(f"scattered{par}") for par in range(2)]
        filled = [sem(f"filled{h}") for h in range(HALVES)]
        blk_loaded = [sem(f"blk_loaded{u}") for u in range(UNROLL)]
        blk_stored = [sem(f"blk_stored{u}") for u in range(UNROLL)]
        pair_loaded = [sem("pair_loaded0"), sem("pair_loaded1")]
        fin_stored = [sem("fin_stored0"), sem("fin_stored1")]
        c_pool, c_dve, c_pe, c_act = sem("c_pool"), sem("c_dve"), sem("c_pe"), sem("c_act")
        pe_xT, pe_q, pe_k, pe_v, pe_fq, pe_fk = (sem(n) for n in ("pe_xT", "pe_q", "pe_k", "pe_v", "pe_fq", "pe_fk"))
        pe_kT, pe_kv, pe_att, pe_attT, pe_wo = (sem(n) for n in ("pe_kT", "pe_kv", "pe_att", "pe_attT", "pe_wo"))
        pe_x2T, pe_logit, pe_place = (sem(n) for n in ("pe_x2T", "pe_logit", "pe_place"))
        ac_xT, ac_q2, ac_k2, ac_fq, ac_fk, ac_kT = (sem(n) for n in ("ac_xT", "ac_q2", "ac_k2", "ac_fq", "ac_fk", "ac_kT"))
        ac_attT, ac_x2T, ac_rows, ac_exp8 = (sem(n) for n in ("ac_attT", "ac_x2T", "ac_rows", "ac_exp8"))
        dv_v, dv_kv, dv_den, dv_z, dv_att = (sem(n) for n in ("dv_v", "dv_kv", "dv_den", "dv_z", "dv_att"))
        dv_res, dv_stat, dv_mv, dv_eps, pl_rstd, dv_x2 = (sem(n) for n in ("dv_res", "dv_stat", "dv_mv", "dv_eps", "pl_rstd", "dv_x2"))
        dv_top, dv_idx, dv_gap, dv_cho, dv_both = (sem(n) for n in ("dv_top", "dv_idx", "dv_gap", "dv_cho", "dv_both"))
        dv_sum, dv_wd, dv_wd2, dv_w1, dv_pay = (sem(n) for n in ("dv_sum", "dv_wd", "dv_wd2", "dv_w1", "dv_pay"))
        dv_place, dv_pick, dv_slot = (sem(n) for n in ("dv_place", "dv_pick", "dv_slot"))
        tb, fill_ready, table_ready = sem("tb"), sem("fill_ready"), sem("table_ready")
        d_xT, d_h, d_hT, d_y = (sem(n) for n in ("d_xT", "d_h", "d_hT", "d_y"))
        d_xTc, d_silu, d_mul, d_hTc, d_yw, d_pay, d_chain = (sem(n) for n in ("d_xTc", "d_silu", "d_mul", "d_hTc", "d_yw", "d_pay", "d_chain"))
        f_add, f_res, f_stat, f_mv, f_eps, f_rstd, f_fin = (sem(n) for n in ("f_add", "f_res", "f_stat", "f_mv", "f_eps", "f_rstd", "f_fin"))

        x_tok = x.rearrange("(n h) (p t) d -> n p h t d", n=GROUPS, h=2, t=2)

        def x_group(n):
            return x_all[:, n * GT:(n + 1) * GT, :].rearrange("p (h t) d -> p h t d", h=2)

        def live(g):
            return not isinstance(g, int) or 0 <= g < GROUPS

        def first(g):
            return isinstance(g, int) and g == 0

        def bc(ap, axis, shape):
            return ap.unsqueeze(axis).to_broadcast(shape)

        def constants_stand(eng):
            eng.wait_ge(c_dve, 12)

        def known(eng, value):
            return value if isinstance(value, int) else eng.compute_val(value)

        def stage_a_turns(eng, turn):
            def straight(lo, hi, h):
                for i in range(lo, hi):
                    turn(i, h, i % 2)

            def pairs(lo, hi, h):
                with eng.Fori(lo, hi, 2) as i:
                    turn(i, h, lo % 2)
                    turn(i + 1, h, (lo + 1) % 2)

            straight(-1, 4, 0)
            pairs(4, HALF_GROUPS + 2, 0)
            straight(HALF_GROUPS + 2, HALF_GROUPS + 3, 0)
            pairs(HALF_GROUPS + 3, GROUPS - 1, 1)
            straight(GROUPS - 1, GROUPS + 3, 1)

        block = ctx.enter_context(nc.Block())

        @block.sync
        def _(sp):
            small = [(wqT_s, wqT), (wq_s, wq), (wkT_s, wkT), (wk_s, wk), (wvT_s, wvT), (woT_s, woT),
                     (bv_s, bv_rows), (bo_s, bo_rows), (r_s, r_tiled), (bq_s, bq), (bk_s, bk), (router_s, router_wT)]
            sp.dma_start(x_in[:, :, :].rearrange("p (h t) d -> p h t d", h=2), x_tok[0]).then_inc(xg_in, 16)
            for dst, src in small:
                sp.dma_start(dst[:, :], src).then_inc(wts_in, 16)
            for n in range(0, 3):
                sp.dma_start(x_group(n), x_tok[n]).then_inc(x_in_a, 16)
            for n in range(1, 3):
                sp.wait_ge(pe_xT, n)
                sp.dma_start(x_in[:, :, :].rearrange("p (h t) d -> p h t d", h=2), x_tok[n]).then_inc(xg_in, 16)
            for n in range(3, GROUPS):
                sp.dma_start(x_group(n), x_tok[n]).then_inc(x_in_b, 16)
            sp.dma_start(w13_s[:, :, :], w13).then_inc(ffn_in, 16)
            sp.dma_start(w2_s[:, :, :, :], w2).then_inc(ffn_in, 16)
            sp.wait_ge(c_dve, 12)
            for h in range(HALVES):
                lo = h * HALF_ROWS + EXPERTS * REGION
                dst = sorted_rows[lo:lo + UNROLL * P, :].rearrange("(u p) r -> p u r", p=P)
                sp.dma_start(dst, fill_rows[:, HALVES * EXPERTS + h * UNROLL:HALVES * EXPERTS + (h + 1) * UNROLL, :]
                             ).then_inc(dummy_out, 16)
            with sp.Fori(3, GROUPS) as n:
                group = x_tok[bass.ds(n, 1)].rearrange("n p h t d -> (n p) h t d")
                constants_stand(sp)
                sp.wait_ge(pe_xT, n)
                sp.dma_start(x_in[:, :, :].rearrange("p (h t) d -> p h t d", h=2),
                             group).then_inc(xg_in, 16)

            def load_turn(i):
                for u in range(UNROLL):
                    row = sp.value_load(blk_row[0:1, bass.ds(i * UNROLL + u, 1)], min_val=0,
                                        max_val=HALVES * HALF_ROWS - P)
                    if not (isinstance(i, int) and i == 0):
                        transposed = known(sp, (i - 1) * UNROLL + u + 1)
                        read = known(sp, (i - 1) * 2 + (1 if u < UNROLL // 2 else 2))
                        constants_stand(sp)
                        sp.wait_ge(d_xT, transposed)
                        sp.wait_ge(d_pay, read)
                    sp.dma_start(blk_in[:, u, :], sorted_rows[bass.ds(row, P), :]).then_inc(blk_loaded[u], 16)

            sp.wait_ge(dummy_out, 16 * HALVES)
            sp.wait_ge(table_ready, 1)
            sp.wait_ge(filled[0], 16 * EXPERTS)
            load_turn(0)
            with sp.Fori(1, TURNS // 2) as i:
                load_turn(i)
            sp.wait_ge(table_ready, 2)
            sp.wait_ge(filled[1], 16 * EXPERTS)
            with sp.Fori(TURNS // 2, TURNS) as i:
                load_turn(i)

            for u in range(UNROLL):
                sp.wait_ge(blk_stored[u], 16 * TURNS)
            pair = expert_out[0:CHOICES, :].rearrange("(n h p t) d -> n p h (t d)", n=GROUPS, h=2, p=P)

            def load_pair(j, n, again):
                if again:
                    before_last = known(sp, n - 1)
                    constants_stand(sp)
                    sp.wait_ge(f_add, before_last)
                sp.dma_start(pair_in[:, j, :, :, :].rearrange("p h a b -> p h (a b)"), pair[n] if isinstance(n, int)
                             else pair[bass.ds(n, 1)].rearrange("n p h e -> (n p) h e")).then_inc(pair_loaded[j], 16)

            load_pair(0, 0, False)
            load_pair(1, 1, False)
            with sp.Fori(1, GROUPS // 2) as i:
                load_pair(0, i * 2, True)
                load_pair(1, i * 2 + 1, True)
            for j in range(2):
                sp.wait_ge(fin_stored[j], 16 * (GROUPS // 2))

        @block.gpsimd
        def _(pool):
            nc.gpsimd.memset(ident[:, :], 0.0).then_inc(c_pool, 1)
            nc.gpsimd.memset(before[:, :], 1.0).then_inc(c_pool, 1)
            nc.gpsimd.memset(head_mask[:, :, :], 1.0).then_inc(c_pool, 1)
            nc.gpsimd.memset(ones_b[:, :], 1.0)
            nc.gpsimd.memset(minus_half[:, :], -0.5)
            nc.gpsimd.memset(ones8[:, :], 1.0)
            nc.gpsimd.memset(bo_split[:, :, :], 0.0)
            pool.wait_ge(c_pool, 3)
            nc.gpsimd.affine_select(out=ident[:, :], in_=ident[:, :], compare_op=ALU.not_equal, fill=1.0,
                                    base=0, pattern=[[-1, P]], channel_multiplier=1).then_inc(c_pool, 1)
            nc.gpsimd.affine_select(out=before[:, :], in_=before[:, :], compare_op=ALU.is_gt, fill=0.0,
                                    base=0, pattern=[[1, P]], channel_multiplier=-1).then_inc(c_pool, 1)
            nc.gpsimd.affine_select(out=head_mask[:, :, :], in_=head_mask[:, :, :], compare_op=ALU.is_ge, fill=0.0,
                                    base=0, pattern=[[-HEAD_DIM, HEADS], [0, HEAD_DIM]],
                                    channel_multiplier=1).then_inc(c_pool, 1)
            pool.wait_ge(c_pool, 6)
            nc.gpsimd.affine_select(out=head_mask[:, :, :], in_=head_mask[:, :, :], compare_op=ALU.is_ge, fill=0.0,
                                    base=HEAD_DIM - 1, pattern=[[HEAD_DIM, HEADS], [0, HEAD_DIM]],
                                    channel_multiplier=-1).then_inc(c_pool, 1)
            nc.gpsimd.iota(iota_ei[:, :], [[1, EXPERTS]], 0, 0)
            nc.gpsimd.iota(tok2_i[:, :], [[2 * SEQ, BATCHES], [TOP_K, 2]], 0, 2 * TOP_K)
            nc.gpsimd.iota(fill_i[:, :], [[P, FILLS]], CHOICES, 1)
            nc.gpsimd.iota(lane_i[:, :], [[1, 1]], 0, 1)
            for h in range(HALVES):
                nc.gpsimd.iota(region_i[:, h, :], [[REGION, EXPERTS]], h * HALF_ROWS, 0)
                nc.gpsimd.iota(blk_row_i[:, h, :], [[P, BLOCKS]], h * HALF_ROWS, 0)
            nc.gpsimd.iota(blk_i[:, :], [[1, BLOCKS]], 0, 0)
            nc.gpsimd.memset(fill_rows[:, :, :], 0.0).then_inc(c_pool, 1)

            def turn(i, h, par):
                c, d = i - 2, i - 3

                def scatter(t, k):
                    pool.indirect_dma_start(
                        out=sorted_rows[:, :],
                        out_offset=bass.IndirectOffsetOnAxis(
                            ap=slots[:, 1 - par, t, k:k + 1], axis=0),
                        in_=rows_now[:, 1 - par, t, :],
                        in_offset=None).then_inc(scattered[1 - par], 16)

                if live(d):
                    ready = known(pool, d + 1)
                    constants_stand(pool)
                    pool.wait_ge(dv_slot, ready)
                    pool.wait_ge(dv_pay, ready)
                    scatter(0, 0)
                    scatter(0, 1)
                if live(c):
                    pool.wait_ge(dv_eps, c + 1)
                    nc.gpsimd.tensor_tensor(rstd[:, :], var_eps[:, :], minus_half[:, :], ALU.pow).then_inc(pl_rstd, 1)
                if live(d):
                    for t in range(1, GT):
                        scatter(t, 0)
                        scatter(t, 1)
                if isinstance(d, int) and d > 0 and d % HALF_GROUPS == HALF_GROUPS - 1:
                    pool.wait_ge(fill_ready, h + 1)
                    for s in scattered:
                        pool.wait_ge(s, (h + 1) * (16 * HALF_CHOICES // P // 2))
                    for e in range(EXPERTS):
                        pool.indirect_dma_start(
                            out=sorted_rows[:, :],
                            out_offset=bass.IndirectOffsetOnAxis(ap=fill_at[:, h, e:e + 1], axis=0),
                            in_=fill_rows[:, h * EXPERTS + e, :], in_offset=None).then_inc(filled[h], 16)

            pool.wait_ge(c_dve, 12)
            stage_a_turns(pool, turn)

            def store_turn(i):
                for u in range(UNROLL):
                    read = known(pool, i * 2 + (1 if u < UNROLL // 2 else 2))
                    weighted = known(pool, i * UNROLL + u + 1)
                    constants_stand(pool)
                    pool.wait_ge(d_pay, read)
                    pool.wait_ge(d_yw, weighted)
                    pool.indirect_dma_start(
                        out=expert_out[:, :],
                        out_offset=bass.IndirectOffsetOnAxis(ap=blk_dst[:, u:u + 1], axis=0),
                        in_=blk_out[:, u, :], in_offset=None).then_inc(blk_stored[u], 16)

            with pool.Fori(0, TURNS) as i:
                store_turn(i)

            def final(j, n):
                pool.wait_ge(f_eps, n + 1)
                nc.gpsimd.tensor_tensor(rstd[:, :], var_eps[:, :], minus_half[:, :], ALU.pow).then_inc(f_rstd, 1)
            with pool.Fori(0, GROUPS) as n:
                final(0, n)

        @block.scalar
        def _(act):
            act.wait_ge(c_pe, 2)
            nc.scalar.activation(wqrT[:, :], B[0][:, 0:P], ACT.Copy).then_inc(c_act, 1)
            nc.scalar.activation(wkrT[:, :], B[1][:, 0:P], ACT.Copy).then_inc(c_act, 1)
            nc.scalar.activation(bqr[:, :], B[0][:, P:P + 1], ACT.Copy).then_inc(c_act, 1)
            nc.scalar.activation(bkr[:, :], B[1][:, P:P + 1], ACT.Copy).then_inc(c_act, 1)
            act.wait_ge(c_act, 4)

            def turn(i, h, par):
                n, a, b, c = i + 1, i, i - 1, i - 2
                if live(a):
                    act.wait_ge(pe_q, a + 1)
                    nc.scalar.activation(q_sq[:, :], B[1][:, :], ACT.Square, bias=bq_s[:, :]).then_inc(ac_q2, 1)
                if live(b):
                    act.wait_ge(pe_kT, b + 1)
                    nc.scalar.activation(k_tok[:, :, :], B[3][:, :].rearrange("p (t d) -> p t d", t=GT),
                                         ACT.Copy).then_inc(ac_kT, 1)
                if live(a):
                    act.wait_ge(pe_k, a + 1)
                    nc.scalar.activation(k_sq[:, :], B[2][:, :], ACT.Square, bias=bk_s[:, :]).then_inc(ac_k2, 1)
                if live(c):
                    act.wait_ge(pe_x2T, c + 1)
                    nc.scalar.activation(x2T[:, :, :], B[6][:, :].rearrange("p (t d) -> p t d", t=GT),
                                         ACT.Copy).then_inc(ac_x2T, 1)
                if live(a):
                    act.wait_ge(pe_fq, a + 1)
                    if not first(a):
                        act.wait_ge(pe_att, a)
                    nc.scalar.activation(q_feat[:, :], B[1][:, :], ACT.Exp, bias=bqr[:, :]).then_inc(ac_fq, 1)
                if live(c):
                    nc.scalar.activation(x2_all[:, bass.ds(c * GT, GT), :], rows_now[:, par, :, 0:DIM],
                                         ACT.Copy).then_inc(ac_rows, 1)
                if live(a):
                    act.wait_ge(pe_fk, a + 1)
                    nc.scalar.activation(k_feat[:, :], B[2][:, :], ACT.Exp, bias=bkr[:, :]).then_inc(ac_fk, 1)
                if live(b):
                    act.wait_ge(pe_attT, b + 1)
                    nc.scalar.activation(attnT[:, :, :], B[4][:, :].rearrange("p (t d) -> p t d", t=GT),
                                         ACT.Copy).then_inc(ac_attT, 1)
                if live(n):
                    act.wait_ge(pe_xT, n + 1)
                    nc.scalar.activation(xT[:, :], B[0][:, :], ACT.Copy).then_inc(ac_xT, 1)
                if live(c):
                    act.wait_ge(dv_gap, c + 1)
                    nc.scalar.activation(exp8[:, :, :], gap8[:, :, :], ACT.Exp).then_inc(ac_exp8, 1)

            stage_a_turns(act, turn)

            def silu(j, u):
                act.wait_ge(d_h, j + 1)
                nc.scalar.activation(silu_g[:, u % 2, :], B[u % 2][:, 0:INNER], ACT.Silu).then_inc(d_silu, 1)

            def hidden_out(j, u):
                act.wait_ge(d_hT, j + 1)
                nc.scalar.activation(hiddenT[:, u % 2, :], B[2 + u % 2][:, 0:INNER], ACT.Copy).then_inc(d_hTc, 1)

            def expert_turn(i, start):
                for u in range(UNROLL):
                    j = i * UNROLL + u
                    if not (start and u == 0):
                        hidden_out(j - 1, (u - 1) % 2)
                    silu(j, u)

            expert_turn(0, True)
            with act.Fori(1, TURNS) as i:
                expert_turn(i, False)
            hidden_out(TURNS * UNROLL - 1, 1)

            out_v = out.rearrange("(n h) (p t) d -> n p h t d", n=GROUPS, h=2, t=2)
            with act.Fori(0, GROUPS // 2) as i:
                for j in range(2):
                    act.wait_ge(f_fin, i * 2 + j + 1)
                    act.dma_start(out_v[bass.ds(i * 2 + j, 1)].rearrange("n p h t d -> (n p) h t d"),
                                  fin[:, j, :, :].rearrange("p (h t) d -> p h t d", h=2)).then_inc(fin_stored[j], 16)

        @block.vector
        def _(dve):
            dve.wait_ge(c_pool, 8)
            hm = head_mask[:, :, :].rearrange("p h d -> p (h d)")
            nc.vector.tensor_scalar(neg_half_sum[:, :], hm, -0.5 / HEAD_DIM, None, ALU.mult).then_inc(c_dve, 1)
            nc.vector.tensor_copy(iota_e[:, :], iota_ei[:, :]).then_inc(c_dve, 1)
            nc.vector.tensor_copy(tok2_f[:, :], tok2_i[:, :]).then_inc(c_dve, 1)
            nc.vector.tensor_copy(fill_rows[:, :, DIM:DIM + 1], fill_i[:, :].unsqueeze(2)).then_inc(c_dve, 1)
            nc.vector.tensor_copy(lane_f[:, :], lane_i[:, :]).then_inc(c_dve, 1)
            nc.vector.tensor_copy(region_f[:, :, :], region_i[:, :, :]).then_inc(c_dve, 1)
            nc.vector.tensor_copy(blk_f[:, :], blk_i[:, :]).then_inc(c_dve, 1)
            nc.vector.tensor_copy(blk_row_f[:, :, :], blk_row_i[:, :, :]).then_inc(c_dve, 1)
            nc.vector.tensor_copy(place[:, 0, GT, :], region_i[:, 0, :]).then_inc(c_dve, 1)
            nc.vector.tensor_copy(place[:, HALF_GROUPS + 1, GT, :], region_i[:, 1, :]).then_inc(c_dve, 1)
            nc.vector.tensor_copy(kv_den[:, 0, DIM:DIM + HEADS], head_mask[:, :, 0]).then_inc(c_dve, 1)
            nc.vector.tensor_copy(kv_den[:, 1, DIM:DIM + HEADS], head_mask[:, :, 0]).then_inc(c_dve, 1)
            dve.wait_ge(wts_in, 16 * 12)
            nc.vector.scalar_tensor_tensor(blk_r[:, :], r_s[:, :], float(HEAD_DIM) ** -0.5, hm,
                                           ALU.mult, ALU.mult).then_inc(c_dve, 1)
            nc.vector.tensor_copy(bo_split[0:1, :, :], bc(bo_s[0:1, :], 1, [1, GT, DIM])).then_inc(c_dve, 1)
            dve.wait_ge(c_dve, 14)
            nc.vector.tensor_tensor(bo_rest[0:1, 0, :], bo_s[0:1, :], bo_split[0:1, 0, :],
                                    ALU.subtract).then_inc(c_dve, 1)
            dve.wait_ge(c_dve, 15)
            nc.vector.tensor_copy(bo_split[32:33, :, :], bc(bo_rest[0:1, 0, :], 1, [1, GT, DIM])).then_inc(c_dve, 1)
            dve.wait_ge(c_dve, 16)
            nc.vector.tensor_copy(bo_rest[32:33, 0, :], bo_rest[0:1, 0, :]).then_inc(c_dve, 1)
            dve.wait_ge(c_dve, 17)
            nc.vector.tensor_tensor(bo_rest[32:33, 1, :], bo_rest[32:33, 0, :], bo_split[32:33, 0, :],
                                    ALU.subtract).then_inc(c_dve, 1)
            dve.wait_ge(c_dve, 18)
            nc.vector.tensor_copy(bo_split[64:65, :, :], bc(bo_rest[32:33, 1, :], 1, [1, GT, DIM])).then_inc(c_dve, 1)

            grouped = [P, GT, HEADS, HEAD_DIM]

            def turn(i, h, par):
                a, b, c, d = i, i - 1, i - 2, i - 3
                if live(d):
                    dve.wait_ge(pe_place, d + 1)
                    nc.vector.tensor_tensor(
                        place[:, bass.ds(d + h + 1, 1), :, :].rearrange("p a t e -> p (a t) e"),
                        B[7][:, 64:64 + (GT + 1) * EXPERTS].rearrange("p (t e) -> p t e", e=EXPERTS),
                        place[:, bass.ds(d + h, 1), GT, :].to_broadcast([P, GT + 1, EXPERTS]),
                        ALU.add).then_inc(dv_place, 1)
                if live(c):
                    dve.wait_ge(pe_wo, c + 1)
                    if isinstance(c, int) and c < 3:
                        dve.wait_ge(x_in_a, 16 * 3)
                    else:
                        dve.wait_ge(x_in_b, 16 * (GROUPS - 3))
                    nc.vector.tensor_tensor(resid[:, :, :], B[5][:, :].rearrange("p (t d) -> p t d", t=GT),
                                            x_all[:, bass.ds(c * GT, GT), :], ALU.add).then_inc(dv_res, 1)
                if live(d):
                    dve.wait_ge(dv_place, d + 1)
                    nc.vector.tensor_tensor(
                        picked[:, :, :, :], chosen[:, :, :, :],
                        place[:, bass.ds(d + h + 1, 1), 0:GT, :].to_broadcast([P, TOP_K, GT, EXPERTS]),
                        ALU.mult).then_inc(dv_pick, 1)
                if live(c):
                    dve.wait_ge(dv_res, c + 1)
                    for t in range(GT):
                        st = nc.vector.bn_stats(stats[:, t, :], resid[:, t, :])
                    st.then_inc(dv_stat, 1)
                if live(d):
                    dve.wait_ge(dv_pick, d + 1)
                    with nc.allow_low_precision(reason="row numbers are whole and below 2**24"):
                        nc.vector.tensor_reduce(
                            slots[:, 1 - par, :, :].rearrange("p t k -> p k t"),
                            picked[:, :, :, :], AX_X, ALU.add).then_inc(dv_slot, 1)
                if live(c):
                    constants_stand(dve)
                    dve.wait_ge(dv_stat, c + 1)
                    for t in range(GT):
                        st = nc.vector.bn_aggr(meanvar[:, t, :], stats[:, t, :])
                    st.then_inc(dv_mv, 1)
                    dve.wait_ge(dv_mv, c + 1)
                    nc.vector.tensor_scalar(var_eps[:, :], meanvar[:, :, 1], LN_EPS, None, ALU.add).then_inc(dv_eps, 1)
                if live(b):
                    dve.wait_ge(pe_kv, b + 1)
                    nc.vector.tensor_tensor(
                        kv_den[:, :, 0:DIM], B[3][:, 0:2 * DIM].rearrange("p (a d) -> p a d", a=2),
                        bc(hm, 1, [P, 2, DIM]), ALU.mult).then_inc(dv_kv, 1)
                if live(c):
                    dve.wait_ge(pl_rstd, c + 1)
                    if not (isinstance(c, int) and c < 2):
                        dve.wait_ge(ac_rows, c - 1)
                        dve.wait_ge(scattered[par], (c - par) * (8 * TOP_K * GT))
                    for t in range(GT):
                        st = nc.vector.tensor_scalar(rows_now[:, par, t, 0:DIM], resid[:, t, :], meanvar[:, t, 0:1],
                                                     rstd[:, t:t + 1], ALU.subtract, ALU.mult)
                    st.then_inc(dv_x2, 1)
                if live(a):
                    dve.wait_ge(pe_v, a + 1)
                    nc.vector.tensor_tensor(v_tok[:, :, :], B[0][:, :].rearrange("p (t d) -> p t d", t=GT),
                                            bc(bv_s[:, :], 1, [P, GT, DIM]), ALU.add).then_inc(dv_v, 1)
                if live(b):
                    dve.wait_ge(pe_att, b + 1)
                    att = [B[4 + m][:, 0:2 * (DIM + HEADS)].rearrange("p (t d) -> p t d", t=2) for m in range(2)]
                    for m in range(2):
                        st = nc.vector.tensor_scalar(den[:, 2 * m:2 * m + 2, :], att[m][:, :, DIM:DIM + HEADS],
                                                     1e-8, None, ALU.add)
                    st.then_inc(dv_den, 1)
                    dve.wait_ge(dv_den, b + 1)
                    nc.vector.reciprocal(zrec[:, :, :], den[:, :, :]).then_inc(dv_z, 1)
                    dve.wait_ge(dv_z, b + 1)
                    for m in range(2):
                        st = nc.vector.tensor_tensor(
                            attn[:, 2 * m:2 * m + 2, :].rearrange("p t (h e) -> p t h e", h=HEADS),
                            att[m][:, :, 0:DIM].rearrange("p t (h e) -> p t h e", h=HEADS),
                            bc(zrec[:, 2 * m:2 * m + 2, :], 3, [P, 2, HEADS, HEAD_DIM]), ALU.mult)
                    st.then_inc(dv_att, 1)
                if live(c):
                    constants_stand(dve)
                    dve.wait_ge(pe_logit, c + 1)
                    for t in range(GT):
                        st = nc.vector.max(top8[:, t, :], B[7][:, t * EXPERTS:(t + 1) * EXPERTS])
                    st.then_inc(dv_top, 1)
                    constants_stand(dve)
                    dve.wait_ge(dv_top, c + 1)
                    for t in range(GT):
                        st = nc.vector.max_index(idx8[:, t, :], top8[:, t, :], B[7][:, t * EXPERTS:(t + 1) * EXPERTS])
                    st.then_inc(dv_idx, 1)
                    nc.vector.tensor_tensor(gap8[:, :, :], top8[:, :, :], top8[:, :, 0:1].to_broadcast([P, GT, 8]),
                                            ALU.subtract).then_inc(dv_gap, 1)
                    dve.wait_ge(dv_idx, c + 1)
                    nc.vector.tensor_tensor(
                        chosen[:, :, :, :],
                        bc(idx8[:, :, 0:TOP_K].rearrange("p t k -> p k t"), 3, [P, TOP_K, GT, EXPERTS]),
                        iota_e[:, :].unsqueeze(1).unsqueeze(1).to_broadcast([P, TOP_K, GT, EXPERTS]),
                        ALU.is_equal).then_inc(dv_cho, 1)
                    dve.wait_ge(dv_cho, c + 1)
                    nc.vector.tensor_tensor(either[:, :, :], chosen[:, 0, :, :], chosen[:, 1, :, :],
                                            ALU.add).then_inc(dv_both, 1)
                    dve.wait_ge(ac_exp8, c + 1)
                    nc.vector.tensor_reduce(sum8[:, :], exp8[:, :, :], AX_X, ALU.add).then_inc(dv_sum, 1)
                    dve.wait_ge(dv_sum, c + 1)
                    nc.vector.tensor_scalar(wden[:, :], sum8[:, :], 1e-6, 1.0, ALU.mult, ALU.add).then_inc(dv_wd, 1)
                    dve.wait_ge(dv_wd, c + 1)
                    nc.vector.tensor_tensor(wden2[:, :], wden[:, :], exp8[:, :, 1], ALU.add).then_inc(dv_wd2, 1)
                    pay = rows_now[:, par, :, :]
                    nc.vector.tensor_copy(pay[:, :, DIM:DIM + 1], tok2_f[:, bass.ds(c * GT, GT)].unsqueeze(2))
                    nc.vector.tensor_copy(pay[:, :, DIM + 1:DIM + 2], idx8[:, :, 1:2])
                    dve.wait_ge(dv_wd2, c + 1)
                    nc.vector.reciprocal(pay[:, :, DIM + 2:DIM + 3], wden2[:, :].unsqueeze(2)).then_inc(dv_w1, 1)
                    dve.wait_ge(dv_w1, c + 1)
                    nc.vector.scalar_tensor_tensor(pay[:, :, DIM + 3:DIM + 4], exp8[:, :, 1:2], -1.0,
                                                   pay[:, :, DIM + 2:DIM + 3], ALU.add, ALU.mult).then_inc(dv_pay, 1)
                if isinstance(d, int) and d > 0 and d % HALF_GROUPS == HALF_GROUPS - 1:
                    table(h)

            def table(h):
                n = 9 * h
                ends = place[:, (h + 1) * (HALF_GROUPS + 1) - 1, GT, :]
                nc.vector.tensor_scalar(fill_at[:, h, :], ends, lane_f[:, :], None, ALU.add).then_inc(fill_ready, 1)
                nc.vector.tensor_tensor(count_f[:, :], ends, region_f[:, h, :], ALU.subtract).then_inc(tb, 1)
                dve.wait_ge(tb, n + 1)
                nc.vector.tensor_scalar(count_i[:, :], count_f[:, :], float(P - 1), None, ALU.add).then_inc(tb, 1)
                dve.wait_ge(tb, n + 2)
                nc.vector.tensor_scalar(nblk_i[:, :], count_i[:, :], P.bit_length() - 1, None,
                                        ALU.arith_shift_right).then_inc(tb, 1)
                dve.wait_ge(tb, n + 3)
                nc.vector.tensor_copy(nblk_f[:, :], nblk_i[:, :]).then_inc(tb, 1)
                dve.wait_ge(tb, n + 4)
                nc.vector.tensor_tensor_scan(end_f[:, :], ones8[:, :], nblk_f[:, :], 0.0,
                                             ALU.mult, ALU.add).then_inc(tb, 1)
                nc.vector.tensor_scalar(skip_f[:, :], nblk_f[:, :], -float(P), float(REGION),
                                        ALU.mult, ALU.add).then_inc(tb, 1)
                dve.wait_ge(tb, n + 6)
                shape = [P, BLOCKS, EXPERTS]
                nc.vector.tensor_tensor(past[:, :, :], bc(end_f[:, :], 1, shape), bc(blk_f[:, :], 2, shape),
                                        ALU.is_le).then_inc(tb, 1)
                dve.wait_ge(tb, n + 7)
                nc.vector.tensor_tensor(past_skip[:, :, :], past[:, :, :], bc(skip_f[:, :], 1, shape),
                                        ALU.mult).then_inc(tb, 1)
                mine = slice(h * BLOCKS, (h + 1) * BLOCKS)
                nc.vector.tensor_reduce(blk_expert[:, mine], past[:, :, :], AX_X, ALU.add)
                dve.wait_ge(tb, n + 8)
                nc.vector.tensor_reduce(blk_skip[:, :], past_skip[:, :, :], AX_X, ALU.add).then_inc(tb, 1)
                dve.wait_ge(tb, n + 9)
                nc.vector.tensor_scalar(blk_expert_i[:, mine], blk_expert[:, mine], float(EXPERTS - 1), None, ALU.min)
                nc.vector.tensor_tensor(blk_row[:, mine], blk_skip[:, :], blk_row_f[:, h, :],
                                        ALU.add).then_inc(table_ready, 1)

            stage_a_turns(dve, turn)

            def xT_copy(j, u):
                dve.wait_ge(d_xT, j + 1)
                nc.vector.tensor_copy(blk_xT[:, u % 2, :], B[4 + u % 2][:, 0:P]).then_inc(d_xTc, 1)

            def gate_up(j, u):
                dve.wait_ge(d_silu, j + 1)
                nc.vector.tensor_tensor(hidden[:, u % 2, :], silu_g[:, u % 2, :], B[u % 2][:, INNER:2 * INNER],
                                        ALU.mult).then_inc(d_mul, 1)

            def weigh(j, u, again):
                dve.wait_ge(d_y, j + 1)
                if again is not None:
                    dve.wait_ge(blk_stored[u], again)
                nc.vector.tensor_scalar(blk_out[:, u, :], B[6 + u % 2][:, 0:DIM], blk_w[:, u:u + 1], None,
                                        ALU.mult).then_inc(d_yw, 1)

            def payload(i, part, start):
                s = slice(part * UNROLL // 2, (part + 1) * UNROLL // 2)
                for u in range(s.start, s.stop):
                    dve.wait_ge(blk_loaded[u], 16 * (i + 1))
                    if not start:
                        dve.wait_ge(blk_stored[u], 16 * i)
                nc.vector.tensor_tensor(is_second[:, s], blk_in[:, s, DIM + 1],
                                        blk_expert[:, bass.ds(i * UNROLL + s.start, UNROLL // 2)],
                                        ALU.is_equal).then_inc(d_chain, 1)
                dve.wait_ge(d_chain, (i * 2 + part) * 2 + 1)
                nc.vector.tensor_tensor(w_diff[:, s], is_second[:, s], blk_in[:, s, DIM + 3],
                                        ALU.mult).then_inc(d_chain, 1)
                nc.vector.tensor_tensor(blk_dst[:, s], is_second[:, s], blk_in[:, s, DIM], ALU.add)
                dve.wait_ge(d_chain, (i * 2 + part) * 2 + 2)
                nc.vector.tensor_tensor(blk_w[:, s], w_diff[:, s], blk_in[:, s, DIM + 2],
                                        ALU.add).then_inc(d_pay, 1)

            def expert_turn(i, start, end):
                if start:
                    dve.wait_ge(blk_loaded[0], 16)
                    xT_copy(0, 0)
                for u in range(UNROLL):
                    j = i * UNROLL + u
                    if not (start and u < 2):
                        su = (u - 2) % UNROLL
                        again = None if (start or (u < 2 and isinstance(i, int) and i == 1)) else \
                            (16 * i if u >= 2 else 16 * (i - 1))
                        if su == 0:
                            dve.wait_ge(d_pay, 2 * i + 1)
                        elif su == 4:
                            dve.wait_ge(d_pay, 2 * i + 2)
                        weigh(j - 2, su, again)
                    if not (end and u == UNROLL - 1):
                        xT_copy(j + 1, u + 1)
                    if u == 1:
                        payload(i, 0, start)
                    if u == 5:
                        payload(i, 1, start)
                    gate_up(j, u)

            expert_turn(0, True, False)
            expert_turn(1, False, False)
            with dve.Fori(2, TURNS - 1) as i:
                expert_turn(i, False, False)
            expert_turn(TURNS - 1, False, True)
            weigh(TURNS * UNROLL - 2, UNROLL - 2, 16 * (TURNS - 1))
            weigh(TURNS * UNROLL - 1, UNROLL - 1, 16 * (TURNS - 1))

            def final(i, j, again):
                n = i * 2 + j
                dve.wait_ge(pair_loaded[j], 16 * (i + 1))
                pr = pair_in[:, j, :, :, :].rearrange("p h t (k d) -> p (h t) k d", k=TOP_K)
                nc.vector.tensor_tensor(attn[:, :, :], pr[:, :, 0, :], pr[:, :, 1, :], ALU.add).then_inc(f_add, 1)
                dve.wait_ge(f_add, n + 1)
                nc.vector.tensor_tensor(resid[:, :, :], attn[:, :, :], x2_all[:, bass.ds(n * GT, GT), :],
                                        ALU.add).then_inc(f_res, 1)
                dve.wait_ge(f_res, n + 1)
                for t in range(GT):
                    st = nc.vector.bn_stats(stats[:, t, :], resid[:, t, :])
                st.then_inc(f_stat, 1)
                constants_stand(dve)
                dve.wait_ge(f_stat, n + 1)
                for t in range(GT):
                    st = nc.vector.bn_aggr(meanvar[:, t, :], stats[:, t, :])
                st.then_inc(f_mv, 1)
                dve.wait_ge(f_mv, n + 1)
                nc.vector.tensor_scalar(var_eps[:, :], meanvar[:, :, 1], LN_EPS, None, ALU.add).then_inc(f_eps, 1)
                if again:
                    dve.wait_ge(fin_stored[j], 16 * i)
                dve.wait_ge(f_rstd, n + 1)
                for t in range(GT):
                    st = nc.vector.tensor_scalar(fin[:, j, t, :], resid[:, t, :], meanvar[:, t, 0:1],
                                                 rstd[:, t:t + 1], ALU.subtract, ALU.mult)
                st.then_inc(f_fin, 1)

            final(0, 0, False)
            final(0, 1, False)
            with dve.Fori(1, GROUPS // 2) as i:
                final(i, 0, True)
                final(i, 1, True)

        @block.tensor
        def _(pe):
            pe.wait_ge(wts_in, 16 * 12)
            pe.wait_ge(c_dve, 13)
            nc.tensor.matmul(B[0][:, 0:P], wq_s[:, :], blk_r[:, :], start=True, stop=True)
            nc.tensor.matmul(B[0][:, P:P + 1], blk_r[:, :], bq_s[:, :], start=True, stop=True).then_inc(c_pe, 1)
            nc.tensor.matmul(B[1][:, 0:P], wk_s[:, :], blk_r[:, :], start=True, stop=True)
            nc.tensor.matmul(B[1][:, P:P + 1], blk_r[:, :], bk_s[:, :], start=True, stop=True).then_inc(c_pe, 1)
            pe.wait_ge(c_act, 4)
            pe.wait_ge(c_dve, 19)

            def turn(i, h, par):
                n, a, b, c = i + 1, i, i - 1, i - 2
                if live(a):
                    pe.wait_ge(ac_xT, a + 1)
                    if not first(a):
                        pe.wait_ge(ac_fq, a)
                    nc.tensor.matmul(B[1][:, :], wqT_s[:, :], xT[:, :], start=True, stop=True).then_inc(pe_q, 1)
                if live(b):
                    pe.wait_ge(ac_fk, b + 1)
                    if not first(b):
                        pe.wait_ge(dv_kv, b)
                    for t in range(GT):
                        mm = nc.tensor.transpose(B[3][:, t * P:(t + 1) * P], k_feat[:, t * P:(t + 1) * P], ident[:, :])
                    mm.then_inc(pe_kT, 1)
                if live(a):
                    if not first(a):
                        pe.wait_ge(ac_fk, a)
                    nc.tensor.matmul(B[2][:, :], wkT_s[:, :], xT[:, :], start=True, stop=True).then_inc(pe_k, 1)
                if live(b):
                    pe.wait_ge(ac_kT, b + 1)
                    pe.wait_ge(dv_v, b + 1)
                    for m in range(2):
                        for t in range(2):
                            mm = nc.tensor.matmul(B[3][:, m * DIM:(m + 1) * DIM], k_tok[:, 2 * m + t, :],
                                                  v_tok[:, 2 * m + t, :], start=(t == 0), stop=(t == 1))
                    mm.then_inc(pe_kv, 1)
                if live(a):
                    pe.wait_ge(ac_q2, a + 1)
                    nc.tensor.matmul(B[1][:, :], wqrT[:, :], xT[:, :], start=True, stop=False)
                    nc.tensor.matmul(B[1][:, :], neg_half_sum[:, :], q_sq[:, :], start=False, stop=True).then_inc(pe_fq, 1)
                    for t in range(GT):
                        mm = nc.tensor.matmul(B[0][:, t * P:(t + 1) * P], xT[:, t * P:(t + 1) * P], wvT_s[:, :],
                                              start=True, stop=True)
                    mm.then_inc(pe_v, 1)
                if live(c):
                    pe.wait_ge(dv_x2, c + 1)
                    if not first(c):
                        pe.wait_ge(ac_x2T, c)
                    for t in range(GT):
                        mm = nc.tensor.transpose(B[6][:, t * P:(t + 1) * P], rows_now[:, par, t, 0:DIM], ident[:, :])
                    mm.then_inc(pe_x2T, 1)
                if live(b):
                    pe.wait_ge(ac_fq, b + 1)
                    pe.wait_ge(dv_kv, b + 1)
                    if not first(b):
                        pe.wait_ge(ac_attT, b)
                        pe.wait_ge(dv_res, b)
                    for t in range(GT):
                        mm = nc.tensor.matmul(B[4 + t // 2][:, (t % 2) * (DIM + HEADS):(t % 2 + 1) * (DIM + HEADS)],
                                              q_feat[:, t * P:(t + 1) * P], kv_den[:, t // 2, :], start=True, stop=True)
                    mm.then_inc(pe_att, 1)
                if live(a):
                    pe.wait_ge(ac_k2, a + 1)
                    nc.tensor.matmul(B[2][:, :], wkrT[:, :], xT[:, :], start=True, stop=False)
                    nc.tensor.matmul(B[2][:, :], neg_half_sum[:, :], k_sq[:, :], start=False, stop=True).then_inc(pe_fk, 1)
                if live(c):
                    pe.wait_ge(ac_x2T, c + 1)
                    if not first(c):
                        pe.wait_ge(dv_place, c)
                    for t in range(GT):
                        mm = nc.tensor.matmul(B[7][:, t * EXPERTS:(t + 1) * EXPERTS], x2T[:, t, :], router_s[:, :],
                                              start=True, stop=True)
                    mm.then_inc(pe_logit, 1)
                if live(b):
                    pe.wait_ge(dv_att, b + 1)
                    for t in range(GT):
                        mm = nc.tensor.transpose(B[4][:, t * P:(t + 1) * P], attn[:, t, :], ident[:, :])
                    mm.then_inc(pe_attT, 1)
                if live(n):
                    pe.wait_ge(xg_in, 16 * (n + 1))
                    if live(a):
                        pe.wait_ge(dv_v, a + 1)
                    for t in range(GT):
                        mm = nc.tensor.transpose(B[0][:, t * P:(t + 1) * P], x_in[:, t, :], ident[:, :])
                    mm.then_inc(pe_xT, 1)
                if live(b):
                    pe.wait_ge(ac_attT, b + 1)
                    nc.tensor.matmul(B[5][:, :], ones_b[:, :], bo_split[:, :, :].rearrange("p t d -> p (t d)"),
                                     start=True, stop=False)
                    for t in range(GT):
                        mm = nc.tensor.matmul(B[5][:, t * P:(t + 1) * P], attnT[:, t, :], woT_s[:, :],
                                              start=False, stop=(t == GT - 1))
                    mm.then_inc(pe_wo, 1)
                if live(c):
                    pe.wait_ge(dv_both, c + 1)
                    at = 64
                    nc.tensor.matmul(B[7][:, at:at + GT * EXPERTS], before[:, :],
                                     either[:, :, :].rearrange("p t e -> p (t e)"), start=True, stop=False,
                                     skip_group_check=True)
                    for t in range(GT):
                        lo = (t + 1) * EXPERTS
                        mm = nc.tensor.matmul(B[7][:, at + lo:at + (GT + 1) * EXPERTS], ones_b[:, :],
                                              either[:, 0:GT - t, :].rearrange("p t e -> p (t e)"),
                                              start=False, stop=(t == GT - 1), skip_group_check=True)
                    mm.then_inc(pe_place, 1)

            stage_a_turns(pe, turn)

            def expert_of(j):
                return pe.value_load(blk_expert_i[0:1, bass.ds(j, 1)], min_val=0, max_val=EXPERTS - 1)

            def xT_blk(i, u, start):
                j = i * UNROLL + u
                pe.wait_ge(blk_loaded[u], 16 * (i + 1))
                if not start:
                    pe.wait_ge(d_xTc, j - 1)
                nc.tensor.transpose(B[4 + u % 2][:, 0:P], blk_in[:, u, 0:DIM], ident[:, :]).then_inc(d_xT, 1)

            def up(j, u, e, start):
                pe.wait_ge(d_xTc, j + 1)
                if not start:
                    pe.wait_ge(d_mul, j - 1)
                nc.tensor.matmul(B[u % 2][:, :], blk_xT[:, u % 2, :],
                                 w13_s[:, bass.ds(e, 1), :].rearrange("p a i -> p (a i)"),
                                 start=True, stop=True).then_inc(d_h, 1)

            def hidT(j, u, start):
                pe.wait_ge(d_mul, j + 1)
                if not start:
                    pe.wait_ge(d_hTc, j - 1)
                for c in range(2):
                    mm = nc.tensor.transpose(B[2 + u % 2][:, c * P:(c + 1) * P], hidden[:, u % 2, c * P:(c + 1) * P],
                                             ident[:, :])
                mm.then_inc(d_hT, 1)

            def down(j, u, e, start):
                pe.wait_ge(d_hTc, j + 1)
                if not start:
                    pe.wait_ge(d_yw, j - 1)
                for c in range(2):
                    mm = nc.tensor.matmul(B[6 + u % 2][:, 0:DIM], hiddenT[:, u % 2, c * P:(c + 1) * P],
                                          w2_s[:, bass.ds(e, 1), c, :].rearrange("p a d -> p (a d)"),
                                          start=(c == 0), stop=(c == 1))
                mm.then_inc(d_y, 1)

            def expert_turn(i, start, end):
                es = {u: expert_of(i * UNROLL + u) for u in range(UNROLL)}
                if start:
                    xT_blk(0, 0, True)
                else:
                    es[-2], es[-1] = expert_of(i * UNROLL - 2), expert_of(i * UNROLL - 1)
                for u in range(UNROLL):
                    j = i * UNROLL + u
                    up(j, u, es[u], start and u < 2)
                    if not (start and u < 2):
                        down(j - 2, u, es[u - 2], start and u < 4)
                    if not (end and u == UNROLL - 1):
                        if u == UNROLL - 1:
                            xT_blk(i + 1, 0, False)
                        else:
                            xT_blk(i, u + 1, start and u == 0)
                    if not (start and u == 0):
                        hidT(j - 1, u + 1, start and u < 3)

            pe.wait_ge(ffn_in, 32)
            pe.wait_ge(table_ready, 1)
            expert_turn(0, True, False)
            with pe.Fori(1, TURNS // 2) as i:
                expert_turn(i, False, False)
            pe.wait_ge(table_ready, 2)
            with pe.Fori(TURNS // 2, TURNS - 1) as i:
                expert_turn(i, False, False)
            expert_turn(TURNS - 1, False, True)
            last = TURNS * UNROLL - 1
            el = expert_of(last - 1), expert_of(last)
            down(last - 1, 0, el[0], False)
            hidT(last, 1, False)
            down(last, 1, el[1], False)


def kernel(**inputs):
    import numpy as _np
    import concourse.bacc as _bacc
    from concourse import mybir as _mybir
    from concourse.bass_utils import run_bass_kernel_spmd as _run

    get = {k: _np.asarray(v) for k, v in inputs.items()}
    wq, wk, wv, wo = (get["L0_attn_W" + c] for c in "qkvo")
    bq, bk, bv, bo = (get["L0_attn_b" + c] for c in "qkvo")
    h, e = HEADS, HEAD_DIM
    laid = {
        "x": get["L0_attn_x"], "wqT": wq.T, "wq": wq, "bq": bq.reshape(P, 1),
        "wkT": wk.T, "wk": wk, "bk": bk.reshape(P, 1), "wvT": wv.T,
        "bv_rows": _np.broadcast_to(bv, (P, DIM)), "woT": wo.T, "bo_rows": _np.broadcast_to(bo, (P, DIM)),
        "r_tiled": _np.broadcast_to(get["L0_attn_R"][None, :, None, :], (h, e, h, e)).reshape(P, P),
        "router_wT": get["L0_ffn_router_w"].T,
        "w13": get["L0_ffn_w13"].transpose(1, 0, 2),
        "w2": get["L0_ffn_w2"].reshape(EXPERTS, 2, P, DIM).transpose(2, 0, 1, 3),
    }
    nc = _bacc.Bacc("TRN2", target_bir_lowering=False, num_devices=1)
    arrays, args = {}, []
    for name, a in laid.items():
        a = _np.ascontiguousarray(a)
        arrays[f"in_{name}"] = a
        args.append(nc.dram_tensor(f"in_{name}", a.shape, _mybir.dt.from_np(a.dtype), kind="ExternalInput").ap())
    args.append(nc.dram_tensor("out_0", (BATCHES, SEQ, DIM), _mybir.dt.float32, kind="ExternalOutput").ap())
    moe_kernel(nc, *args)
    r = _run(nc, [arrays], core_ids=[0])
    return r.results[0]["out_0"]
```

```python
from contextlib import ExitStack

import numpy as np

import concourse.bass as bass
from concourse import mybir

ALU = mybir.AluOpType
ACT = mybir.ActivationFunctionType
F32 = mybir.dt.float32
F32R = mybir.dt.float32r
BF16 = mybir.dt.bfloat16
U32 = mybir.dt.uint32
I32 = mybir.dt.int32
AX_X = mybir.AxisListType.X

P = 128
DIM = 128
HEADS = 16
HEAD_DIM = DIM // HEADS
BATCHES, SEQ = 32, 256
TOKENS = BATCHES * SEQ
EXPERTS = 8
INNER = 256
TOP_K = 2
LN_EPS = 1e-5

GT = 4
GROUPS = TOKENS // (GT * P)
TILES = TOKENS // P
HALVES = 2
HALF_GROUPS = GROUPS // HALVES
CONSTANTS = 10
PAYLOAD = 4
ROW = DIM + PAYLOAD
CHOICES = TOP_K * TOKENS
HALF_CHOICES = CHOICES // HALVES
UNROLL = 12
BLOCKS = -(-(HALF_CHOICES // P + EXPERTS - 1) // UNROLL) * UNROLL
REGION = TOKENS // HALVES + P
HALF_ROWS = EXPERTS * REGION + UNROLL * P
FILLS = HALVES * (EXPERTS + UNROLL)
TURNS = HALVES * BLOCKS // UNROLL
LEAD = 4
HALF_PAIRS = HALF_GROUPS // 2
FIRST_PAIRS = TURNS // 2 + 1


def moe_kernel(nc, x, weights_fold, weights_rest, w13, w2, out):
    with ExitStack() as ctx:
        def sb(name, shape, dt=F32):
            return ctx.enter_context(nc.sbuf_tensor(name, shape, dt))

        def bank(name, shape, dt=F32):
            return ctx.enter_context(nc.psum_tensor(name, shape, dt))

        def sem(name):
            return ctx.enter_context(nc.semaphore(name))

        sorted_rows = nc.dram_tensor("sorted_rows", [HALVES * HALF_ROWS, ROW], F32, kind="Internal").ap()
        expert_out = nc.dram_tensor("expert_out", [CHOICES + FILLS * P, DIM], F32, kind="Internal").ap()

        fold_s = sb("fold_s", [P, 3 * DIM + 2])
        r_s, wq_s, wk_s = (fold_s[:, n * DIM:(n + 1) * DIM] for n in range(3))
        bq_s, bk_s = fold_s[:, 3 * DIM:3 * DIM + 1], fold_s[:, 3 * DIM + 1:3 * DIM + 2]
        rest_s = sb("rest_s", [P, 6 * DIM + EXPERTS])
        wqT_s, wkT_s, wvT_s, woT_s, bv_s, bo_s = (rest_s[:, n * DIM:(n + 1) * DIM] for n in range(6))
        router_in = rest_s[:, 6 * DIM:6 * DIM + EXPERTS]
        router_s = sb("router_s", [P, EXPERTS])
        w13_s = sb("w13_s", [P, EXPERTS, 2 * INNER])
        w13_hi = sb("w13_hi", [P, EXPERTS, 2 * INNER], F32R)
        w13_lo = sb("w13_lo", [P, EXPERTS, 2 * INNER], F32R)
        w2_s = sb("w2_s", [P, EXPERTS, 2, DIM])
        ident = sb("ident", [P, P])
        head_mask = sb("head_mask", [P, HEADS, HEAD_DIM])
        neg_half_sum = sb("neg_half_sum", [P, P])
        blk_r = sb("blk_r", [P, P])
        wqrT, wkrT = sb("wqrT", [P, P]), sb("wkrT", [P, P])
        bqr, bkr = sb("bqr", [P, 1]), sb("bkr", [P, 1])
        before = sb("before", [P, P], BF16)
        ones_b = sb("ones_b", [P, P], BF16)
        bo_split = sb("bo_split", [P, GT, DIM], BF16)
        bo_rest = sb("bo_rest", [P, 2, DIM])
        iota_e = sb("iota_e", [P, EXPERTS], U32)
        iota_ei = sb("iota_ei", [P, EXPERTS], I32)
        minus_half = sb("minus_half", [P, GT])
        tok2_i = sb("tok2_i", [P, TILES], I32)
        fill_i = sb("fill_i", [P, FILLS], I32)
        fill_rows = sb("fill_rows", [P, FILLS, ROW])
        region_i = sb("region_i", [P, HALVES, EXPERTS], I32)
        region_f = sb("region_f", [P, HALVES, EXPERTS])
        blk_i = sb("blk_i", [P, BLOCKS], I32)
        blk_f = sb("blk_f", [P, BLOCKS])
        blk_row_i = sb("blk_row_i", [P, HALVES, BLOCKS], I32)
        blk_row_f = sb("blk_row_f", [P, HALVES, BLOCKS])
        ones8 = sb("ones8", [P, EXPERTS])

        x_all = sb("x_all", [P, TILES, DIM])
        x_in = sb("x_in", [P, GT, DIM])
        xT = sb("xT", [P, GT * P])
        q_sq, k_sq = sb("q_sq", [P, GT * P]), sb("k_sq", [P, GT * P])
        q_feat, k_feat = sb("q_feat", [P, GT * P]), sb("k_feat", [P, GT * P])
        k_tok = sb("k_tok", [P, GT, DIM])
        v_tok = sb("v_tok", [P, GT, DIM])
        kv_den = sb("kv_den", [P, 2, DIM + HEADS])
        den = sb("den", [P, GT, HEADS])
        zrec = sb("zrec", [P, GT, HEADS])
        attn = sb("attn", [P, GT, DIM])
        attnT = sb("attnT", [P, GT, P])
        resid = sb("resid", [P, GT, DIM])
        stats = sb("stats", [P, GT, 6])
        meanvar = sb("meanvar", [P, GT, 2])
        var_eps = sb("var_eps", [P, GT])
        rstd = sb("rstd", [P, GT])
        shift = sb("shift", [P, GT])
        x2T = sb("x2T", [P, GT, P])
        rows_now = sb("rows_now", [P, 2, GT, ROW])
        tok2_f = sb("tok2_f", [P, TILES])
        top8 = sb("top8", [P, GT, 8])
        idx8 = sb("idx8", [P, GT, 8], U32)
        gap8 = sb("gap8", [P, GT, 8])
        exp8 = sb("exp8", [P, GT, 8])
        sum8 = sb("sum8", [P, GT])
        wden = sb("wden", [P, GT])
        wden2 = sb("wden2", [P, GT])
        chosen = sb("chosen", [P, TOP_K, GT, EXPERTS], BF16)
        either = sb("either", [P, GT, EXPERTS], BF16)
        place = sb("place", [P, GROUPS + HALVES, GT + 1, EXPERTS])
        picked = sb("picked", [P, TOP_K, GT, EXPERTS])
        slots = sb("slots", [P, 2, GT, TOP_K], U32)

        fill_at = sb("fill_at", [P, HALVES, EXPERTS], I32)
        count_f = sb("count_f", [P, EXPERTS])
        count_i = sb("count_i", [P, EXPERTS], I32)
        nblk_i = sb("nblk_i", [P, EXPERTS], I32)
        nblk_f = sb("nblk_f", [P, EXPERTS])
        end_f = sb("end_f", [P, EXPERTS])
        skip_f = sb("skip_f", [P, EXPERTS])
        past = sb("past", [P, BLOCKS, EXPERTS])
        past_skip = sb("past_skip", [P, BLOCKS, EXPERTS])
        blk_skip = sb("blk_skip", [P, BLOCKS])
        blk_expert = sb("blk_expert", [P, HALVES * BLOCKS])
        blk_expert_i = sb("blk_expert_i", [P, LEAD + HALVES * BLOCKS], I32)
        blk_row = sb("blk_row", [P, HALVES * BLOCKS], I32)

        blk_in = sb("blk_in", [P, UNROLL, ROW])
        blk_xT_hi = sb("blk_xT_hi", [P, 2, P], F32R)
        blk_xT_lo = sb("blk_xT_lo", [P, 2, P], F32R)
        silu_g = sb("silu_g", [P, 2, INNER])
        hidden = sb("hidden", [P, 2, INNER])
        hiddenT = sb("hiddenT", [P, 2, INNER])
        blk_out = sb("blk_out", [P, UNROLL, DIM])
        is_second = sb("is_second", [P, UNROLL])
        w_diff = sb("w_diff", [P, UNROLL])
        blk_w = sb("blk_w", [P, UNROLL])
        blk_dst = sb("blk_dst", [P, UNROLL], U32)

        pair_in = sb("pair_in", [P, 2, 2, TOP_K, 2 * DIM])
        total = sb("total", [P, 2, GT, DIM])
        stats2 = sb("stats2", [P, 2, GT, 6])
        meanvar2 = sb("meanvar2", [P, 2, GT, 2])
        var_eps2 = sb("var_eps2", [P, 2, GT])
        rstd2 = sb("rstd2", [P, 2, GT])
        shift2 = sb("shift2", [P, 2, GT])
        fin = sb("fin", [P, 2, GT, DIM])

        B = [bank(f"bank{n}", [P, 512]) for n in range(8)]

        fold_in, rest_in, xg_in = sem("fold_in"), sem("rest_in"), sem("xg_in")
        w13_in, w2_in, w13_h, w13_l = sem("w13_in"), sem("w2_in"), sem("w13_h"), sem("w13_l")
        x_in_a, x_in_b = sem("x_in_a"), sem("x_in_b")
        fill_rows_ready, dummy_out = sem("fill_rows_ready"), sem("dummy_out")
        scattered = [sem(f"scattered{par}") for par in range(2)]
        filled = [sem(f"filled{h}") for h in range(HALVES)]
        blk_loaded = [sem(f"blk_loaded{u}") for u in range(UNROLL)]
        blk_stored = [sem(f"blk_stored{u}") for u in range(UNROLL)]
        pair_loaded = [sem("pair_loaded0"), sem("pair_loaded1")]
        fin_stored = [sem("fin_stored0"), sem("fin_stored1")]
        c_pool, c_dve, c_pe, c_act = sem("c_pool"), sem("c_dve"), sem("c_pe"), sem("c_act")
        pe_xT, pe_q, pe_k, pe_v, pe_fq, pe_fk = (sem(n) for n in ("pe_xT", "pe_q", "pe_k", "pe_v", "pe_fq", "pe_fk"))
        pe_kT, pe_kv, pe_att, pe_attT, pe_wo = (sem(n) for n in ("pe_kT", "pe_kv", "pe_att", "pe_attT", "pe_wo"))
        pe_x2T, pe_logit, pe_place = (sem(n) for n in ("pe_x2T", "pe_logit", "pe_place"))
        ac_xT, ac_q2, ac_k2, ac_fq, ac_fk, ac_kT = (sem(n) for n in ("ac_xT", "ac_q2", "ac_k2", "ac_fq", "ac_fk", "ac_kT"))
        ac_attT, ac_x2T, ac_rows, ac_exp8 = (sem(n) for n in ("ac_attT", "ac_x2T", "ac_rows", "ac_exp8"))
        dv_v, dv_kv, dv_den, dv_z, dv_att = (sem(n) for n in ("dv_v", "dv_kv", "dv_den", "dv_z", "dv_att"))
        dv_res, dv_stat, dv_mv, dv_eps, pl_rstd, dv_shift = (sem(n) for n in ("dv_res", "dv_stat", "dv_mv", "dv_eps", "pl_rstd", "dv_shift"))
        dv_top, dv_idx, dv_gap, dv_cho, dv_both = (sem(n) for n in ("dv_top", "dv_idx", "dv_gap", "dv_cho", "dv_both"))
        dv_sum, dv_wd, dv_wd2, dv_w1, dv_pay = (sem(n) for n in ("dv_sum", "dv_wd", "dv_wd2", "dv_w1", "dv_pay"))
        dv_place, dv_pick, dv_slot = (sem(n) for n in ("dv_place", "dv_pick", "dv_slot"))
        tb, fill_ready, table_ready = sem("tb"), sem("fill_ready"), sem("table_ready")
        d_xT, d_h, d_hT, d_y = (sem(n) for n in ("d_xT", "d_h", "d_hT", "d_y"))
        d_xTh, d_xTc, d_silu, d_mul, d_hTc, d_yw, d_pay, d_chain = (sem(n) for n in ("d_xTh", "d_xTc", "d_silu", "d_mul", "d_hTc", "d_yw", "d_pay", "d_chain"))
        f_add, f_stat, f_mv, f_eps, f_rstd, f_shift, f_fin = (sem(n) for n in ("f_add", "f_stat", "f_mv", "f_eps", "f_rstd", "f_shift", "f_fin"))

        x_tok = x.rearrange("(n h) (p t) d -> n p h t d", n=GROUPS, h=2, t=2)

        def x_group(n):
            return x_all[:, n * GT:(n + 1) * GT, :].rearrange("p (h t) d -> p h t d", h=2)

        def live(g):
            return not isinstance(g, int) or 0 <= g < GROUPS

        def first(g):
            return isinstance(g, int) and g == 0

        def bc(ap, axis, shape):
            return ap.unsqueeze(axis).to_broadcast(shape)

        def constants_stand(eng):
            eng.wait_ge(c_dve, CONSTANTS)

        def known(eng, value):
            return value if isinstance(value, int) else eng.compute_val(value)

        def stage_a_turns(eng, turn):
            def straight(lo, hi, h):
                for i in range(lo, hi):
                    turn(i, h, i % 2)

            def pairs(lo, hi, h):
                with eng.Fori(lo, hi, 2) as i:
                    turn(i, h, lo % 2)
                    turn(i + 1, h, (lo + 1) % 2)

            straight(-1, 4, 0)
            pairs(4, HALF_GROUPS + 2, 0)
            straight(HALF_GROUPS + 2, HALF_GROUPS + 3, 0)
            pairs(HALF_GROUPS + 3, GROUPS - 1, 1)
            straight(GROUPS - 1, GROUPS + 3, 1)

        block = ctx.enter_context(nc.Block())

        @block.sync
        def _(sp):
            x_in_v = x_in[:, :, :].rearrange("p (h t) d -> p h t d", h=2)
            sp.dma_start(x_in_v, x_tok[0]).then_inc(xg_in, 16)
            sp.dma_start(fold_s[:, :], weights_fold).then_inc(fold_in, 16)
            sp.dma_start(rest_s[:, :], weights_rest).then_inc(rest_in, 16)
            sp.dma_start(w13_s[:, :, :], w13).then_inc(w13_in, 16)
            sp.wait_ge(pe_xT, 1)
            sp.dma_start(x_in_v, x_tok[1]).then_inc(xg_in, 16)
            for n in range(0, 3):
                sp.dma_start(x_group(n), x_tok[n]).then_inc(x_in_a, 16)
            sp.wait_ge(pe_xT, 2)
            sp.dma_start(x_in_v, x_tok[2]).then_inc(xg_in, 16)
            for n in range(3, GROUPS):
                sp.dma_start(x_group(n), x_tok[n]).then_inc(x_in_b, 16)
            sp.dma_start(w2_s[:, :, :, :], w2).then_inc(w2_in, 16)

            def load_groups(lo, hi):
                with sp.Fori(lo, hi) as n:
                    group = x_tok[bass.ds(n, 1)].rearrange("n p h t d -> (n p) h t d")
                    constants_stand(sp)
                    sp.wait_ge(pe_xT, n)
                    sp.dma_start(x_in_v, group).then_inc(xg_in, 16)

            def fill(h):
                sp.wait_ge(fill_ready, h + 1)
                for s in scattered:
                    sp.wait_ge(s, (h + 1) * (16 * HALF_CHOICES // P // 2))
                starts = nc.values_load_multi_w_load_instructions(
                    fill_at[0:1, h, :], (mybir.EngineType.SP,), min_val=0, max_val=HALVES * HALF_ROWS - P,
                    skip_runtime_bounds_check_because="a region has a block's rows to spare")[1]
                for e in range(EXPERTS):
                    sp.dma_start(sorted_rows[bass.ds(starts[e], P), :], fill_rows[:, h * EXPERTS + e, :]
                                 ).then_inc(filled[h], 16)

            load_groups(3, 5)
            sp.wait_ge(fill_rows_ready, 1)
            for h in range(HALVES):
                lo = h * HALF_ROWS + EXPERTS * REGION
                dst = sorted_rows[lo:lo + UNROLL * P, :].rearrange("(u p) r -> p u r", p=P)
                sp.dma_start(dst, fill_rows[:, HALVES * EXPERTS + h * UNROLL:HALVES * EXPERTS + (h + 1) * UNROLL, :]
                             ).then_inc(dummy_out, 16)
            load_groups(5, HALF_GROUPS + 5)
            fill(0)
            load_groups(HALF_GROUPS + 5, GROUPS)

            def load_turn(i):
                rows = nc.values_load_multi_w_load_instructions(
                    blk_row[0:1, bass.ds(i * UNROLL, UNROLL)], (mybir.EngineType.SP,),
                    min_val=0, max_val=HALVES * HALF_ROWS - P,
                    skip_runtime_bounds_check_because="a block lies in its expert's region or among the stand-ins")[1]
                for u in range(UNROLL):
                    if not (isinstance(i, int) and i == 0):
                        weighted = known(sp, (i - 1) * UNROLL + u + 1)
                        constants_stand(sp)
                        sp.wait_ge(d_yw, weighted)
                    sp.dma_start(blk_in[:, u, :], sorted_rows[bass.ds(rows[u], P), :]).then_inc(blk_loaded[u], 16)

            sp.wait_ge(dummy_out, 16 * HALVES)
            sp.wait_ge(table_ready, 1)
            sp.wait_ge(filled[0], 16 * EXPERTS)
            load_turn(0)
            fill(1)
            with sp.Fori(1, TURNS // 2) as i:
                load_turn(i)
            sp.wait_ge(table_ready, 2)
            sp.wait_ge(filled[1], 16 * EXPERTS)
            load_turn(TURNS // 2)

            pair = expert_out[0:CHOICES, :].rearrange("(n h p t) d -> n p h (t d)", n=GROUPS, h=2, p=P)

            def load_pairs(m):
                for j in range(2):
                    if not (isinstance(m, int) and m == 0):
                        read = known(sp, 2 * m + j - 1)
                        constants_stand(sp)
                        sp.wait_ge(f_add, read)
                    src = pair[2 * m + j] if isinstance(m, int) else \
                        pair[bass.ds(2 * m + j, 1)].rearrange("n p h e -> (n p) h e")
                    sp.dma_start(pair_in[:, j, :, :, :].rearrange("p h a b -> p h (a b)"), src
                                 ).then_inc(pair_loaded[j], 16)

            load_turn(FIRST_PAIRS)
            for u in range(UNROLL):
                sp.wait_ge(blk_stored[u], 16 * (TURNS // 2))
            load_pairs(0)
            with sp.Fori(1, HALF_PAIRS) as m:
                load_turn(FIRST_PAIRS + m)
                load_pairs(m)
            load_turn(TURNS - 1)
            for u in range(UNROLL):
                sp.wait_ge(blk_stored[u], 16 * TURNS)
            with sp.Fori(HALF_PAIRS, 2 * HALF_PAIRS) as m:
                load_pairs(m)
            for j in range(2):
                sp.wait_ge(fin_stored[j], 16 * (GROUPS // 2))

        @block.gpsimd
        def _(pool):
            nc.gpsimd.memset(ident[:, :], 0.0).then_inc(c_pool, 1)
            nc.gpsimd.memset(before[:, :], 1.0).then_inc(c_pool, 1)
            nc.gpsimd.memset(head_mask[:, :, :], 1.0).then_inc(c_pool, 1)
            nc.gpsimd.memset(ones_b[:, :], 1.0)
            nc.gpsimd.memset(minus_half[:, :], -0.5)
            nc.gpsimd.memset(ones8[:, :], 1.0)
            nc.gpsimd.memset(bo_split[:, :, :], 0.0)
            pool.wait_ge(c_pool, 3)
            nc.gpsimd.affine_select(out=ident[:, :], in_=ident[:, :], compare_op=ALU.not_equal, fill=1.0,
                                    base=0, pattern=[[-1, P]], channel_multiplier=1).then_inc(c_pool, 1)
            nc.gpsimd.affine_select(out=before[:, :], in_=before[:, :], compare_op=ALU.is_gt, fill=0.0,
                                    base=0, pattern=[[1, P]], channel_multiplier=-1).then_inc(c_pool, 1)
            nc.gpsimd.affine_select(out=head_mask[:, :, :], in_=head_mask[:, :, :], compare_op=ALU.is_ge, fill=0.0,
                                    base=0, pattern=[[-HEAD_DIM, HEADS], [0, HEAD_DIM]],
                                    channel_multiplier=1).then_inc(c_pool, 1)
            pool.wait_ge(c_pool, 6)
            nc.gpsimd.affine_select(out=head_mask[:, :, :], in_=head_mask[:, :, :], compare_op=ALU.is_ge, fill=0.0,
                                    base=HEAD_DIM - 1, pattern=[[HEAD_DIM, HEADS], [0, HEAD_DIM]],
                                    channel_multiplier=-1).then_inc(c_pool, 1)
            nc.gpsimd.iota(iota_ei[:, :], [[1, EXPERTS]], 0, 0)
            nc.gpsimd.iota(tok2_i[:, :], [[2 * SEQ, BATCHES], [TOP_K, 2]], 0, 2 * TOP_K)
            nc.gpsimd.iota(fill_i[:, :], [[P, FILLS]], CHOICES, 1)
            for h in range(HALVES):
                nc.gpsimd.iota(region_i[:, h, :], [[REGION, EXPERTS]], h * HALF_ROWS, 0)
                nc.gpsimd.iota(blk_row_i[:, h, :], [[P, BLOCKS]], h * HALF_ROWS, 0)
            nc.gpsimd.iota(blk_i[:, :], [[1, BLOCKS]], 0, 0).then_inc(c_pool, 1)
            nc.gpsimd.memset(fill_rows[:, :, :], 0.0).then_inc(c_pool, 1)
            pool.wait_ge(c_pool, 9)
            nc.gpsimd.tensor_copy(fill_rows[:, :, DIM:DIM + 1], fill_i[:, :].unsqueeze(2)).then_inc(fill_rows_ready, 1)

            def turn(i, h, par):
                c, d = i - 2, i - 3

                def scatter(t, k):
                    pool.indirect_dma_start(
                        out=sorted_rows[:, :],
                        out_offset=bass.IndirectOffsetOnAxis(
                            ap=slots[:, 1 - par, t, k:k + 1], axis=0),
                        in_=rows_now[:, 1 - par, t, :],
                        in_offset=None).then_inc(scattered[1 - par], 16)

                if live(c):
                    pool.wait_ge(dv_eps, c + 1)
                    nc.gpsimd.tensor_tensor(rstd[:, :], var_eps[:, :], minus_half[:, :], ALU.pow).then_inc(pl_rstd, 1)
                if live(d):
                    ready = known(pool, d + 1)
                    constants_stand(pool)
                    pool.wait_ge(dv_slot, ready)
                    pool.wait_ge(dv_pay, ready)
                    for t in range(GT):
                        scatter(t, 0)
                        scatter(t, 1)
            pool.wait_ge(c_dve, CONSTANTS)
            stage_a_turns(pool, turn)

            def inverse_std(j, m):
                pool.wait_ge(f_eps, 2 * m + j + 1)
                nc.gpsimd.tensor_tensor(rstd2[:, j, :], var_eps2[:, j, :], minus_half[:, :],
                                        ALU.pow).then_inc(f_rstd, 1)

            def store_turn(i, m=None):
                for u in range(UNROLL):
                    if m is not None and u in (4, 8):
                        inverse_std(u // 4 - 1, m)
                    read = known(pool, i * 2 + (1 if u < UNROLL // 2 else 2))
                    weighted = known(pool, i * UNROLL + u + 1)
                    constants_stand(pool)
                    pool.wait_ge(d_pay, read)
                    pool.wait_ge(d_yw, weighted)
                    pool.indirect_dma_start(
                        out=expert_out[:, :],
                        out_offset=bass.IndirectOffsetOnAxis(ap=blk_dst[:, u:u + 1], axis=0),
                        in_=blk_out[:, u, :], in_offset=None).then_inc(blk_stored[u], 16)

            with pool.Fori(0, FIRST_PAIRS) as i:
                store_turn(i)
            with pool.Fori(0, HALF_PAIRS) as m:
                store_turn(m + FIRST_PAIRS, m)
            store_turn(TURNS - 1)
            with pool.Fori(HALF_PAIRS, 2 * HALF_PAIRS) as m:
                inverse_std(0, m)
                inverse_std(1, m)

        @block.scalar
        def _(act):
            act.wait_ge(c_pe, 2)
            nc.scalar.activation(wqrT[:, :], B[0][:, 0:P], ACT.Copy).then_inc(c_act, 1)
            nc.scalar.activation(wkrT[:, :], B[1][:, 0:P], ACT.Copy).then_inc(c_act, 1)
            nc.scalar.activation(bqr[:, :], B[0][:, P:P + 1], ACT.Copy).then_inc(c_act, 1)
            nc.scalar.activation(bkr[:, :], B[1][:, P:P + 1], ACT.Copy).then_inc(c_act, 1)
            act.wait_ge(rest_in, 16)
            nc.scalar.activation(router_s[:, :], router_in, ACT.Copy, scale=2.0).then_inc(c_act, 1)
            act.wait_ge(c_act, 5)

            def round_weights(experts):
                for e in experts:
                    nc.scalar.activation(w13_hi[:, e, :], w13_s[:, e, :], ACT.Copy, scale=2.0).then_inc(w13_h, 1)

            def turn(i, h, par):
                n, a, b, c = i + 1, i, i - 1, i - 2
                if live(a):
                    act.wait_ge(pe_q, a + 1)
                    nc.scalar.activation(q_sq[:, :], B[1][:, :], ACT.Square, bias=bq_s[:, :]).then_inc(ac_q2, 1)
                if live(b):
                    act.wait_ge(pe_kT, b + 1)
                    nc.scalar.activation(k_tok[:, :, :], B[3][:, :].rearrange("p (t d) -> p t d", t=GT),
                                         ACT.Copy).then_inc(ac_kT, 1)
                if live(a):
                    act.wait_ge(pe_k, a + 1)
                    nc.scalar.activation(k_sq[:, :], B[2][:, :], ACT.Square, bias=bk_s[:, :]).then_inc(ac_k2, 1)
                if live(c):
                    act.wait_ge(dv_shift, c + 1)
                    if not (isinstance(c, int) and c < 2):
                        act.wait_ge(scattered[par], (c - par) * (8 * TOP_K * GT))
                    for t in range(GT):
                        st = nc.scalar.activation(rows_now[:, par, t, 0:DIM], resid[:, t, :], ACT.Identity,
                                                  bias=shift[:, t:t + 1], scale=rstd[:, t:t + 1])
                    st.then_inc(ac_rows, 1)
                if live(a):
                    act.wait_ge(pe_fq, a + 1)
                    if not first(a):
                        act.wait_ge(pe_att, a)
                    nc.scalar.activation(q_feat[:, :], B[1][:, :], ACT.Exp, bias=bqr[:, :]).then_inc(ac_fq, 1)
                if live(c):
                    act.wait_ge(pe_x2T, c + 1)
                    nc.scalar.activation(x2T[:, :, :], B[6][:, :].rearrange("p (t d) -> p t d", t=GT),
                                         ACT.Copy).then_inc(ac_x2T, 1)
                if live(a):
                    act.wait_ge(pe_fk, a + 1)
                    nc.scalar.activation(k_feat[:, :], B[2][:, :], ACT.Exp, bias=bkr[:, :]).then_inc(ac_fk, 1)
                if live(b):
                    act.wait_ge(pe_attT, b + 1)
                    nc.scalar.activation(attnT[:, :, :], B[4][:, :].rearrange("p (t d) -> p t d", t=GT),
                                         ACT.Copy).then_inc(ac_attT, 1)
                if live(n):
                    act.wait_ge(pe_xT, n + 1)
                    nc.scalar.activation(xT[:, :], B[0][:, :], ACT.Copy).then_inc(ac_xT, 1)
                if live(c):
                    act.wait_ge(dv_gap, c + 1)
                    nc.scalar.activation(exp8[:, :, :], gap8[:, :, :], ACT.Exp).then_inc(ac_exp8, 1)
                if isinstance(i, int) and 0 <= i < 4:
                    act.wait_ge(w13_in, 16)
                    round_weights(range(i * EXPERTS // 4, (i + 1) * EXPERTS // 4))

            stage_a_turns(act, turn)

            def silu(j, u):
                act.wait_ge(d_h, j + 1)
                nc.scalar.activation(silu_g[:, u % 2, :], B[u % 2][:, 0:INNER], ACT.Silu).then_inc(d_silu, 1)

            def hidden_out(j, u):
                act.wait_ge(d_hT, j + 1)
                nc.scalar.activation(hiddenT[:, u % 2, :], B[2 + u % 2][:, 0:INNER], ACT.Copy).then_inc(d_hTc, 1)

            def round_x(j, u):
                act.wait_ge(d_xT, j + 1)
                nc.scalar.activation(blk_xT_hi[:, u % 2, :], B[4 + u % 2][:, 0:P], ACT.Copy).then_inc(d_xTh, 1)

            out_v = out.rearrange("(n h) (p t) d -> n p h t d", n=GROUPS, h=2, t=2)

            def finish(j, m):
                g = 2 * m + j
                act.wait_ge(f_shift, g + 1)
                if not (isinstance(m, int) and m == 0):
                    act.wait_ge(fin_stored[j], 16 * m)
                for t in range(GT):
                    st = nc.scalar.activation(fin[:, j, t, :], total[:, j, t, :], ACT.Identity,
                                              bias=shift2[:, j, t:t + 1], scale=rstd2[:, j, t:t + 1])
                st.then_inc(f_fin, 1)
                act.wait_ge(f_fin, g + 1)
                dst = out_v[g] if isinstance(g, int) else out_v[bass.ds(g, 1)].rearrange("n p h t d -> (n p) h t d")
                act.dma_start(dst, fin[:, j, :, :].rearrange("p (h t) d -> p h t d", h=2)).then_inc(fin_stored[j], 16)

            def expert_turn(i, start, end, m=None):
                if start:
                    round_x(0, 0)
                    round_x(1, 1)
                for u in range(UNROLL):
                    j = i * UNROLL + u
                    silu(j, u)
                    if not (end and u >= UNROLL - 2):
                        round_x(j + 2, u)
                    if not (start and u == 0):
                        hidden_out(j - 1, (u - 1) % 2)
                    if m is not None and u in (UNROLL - 3, UNROLL - 1):
                        finish((u - UNROLL + 3) // 2, m)

            expert_turn(0, True, False)
            with act.Fori(1, FIRST_PAIRS) as i:
                expert_turn(i, False, False)
            expert_turn(FIRST_PAIRS, False, False, 0)
            with act.Fori(1, HALF_PAIRS) as m:
                expert_turn(m + FIRST_PAIRS, False, False, m)
            expert_turn(TURNS - 1, False, True)
            hidden_out(TURNS * UNROLL - 1, 1)
            with act.Fori(HALF_PAIRS, 2 * HALF_PAIRS) as m:
                finish(0, m)
                finish(1, m)

        @block.vector
        def _(dve):
            dve.wait_ge(c_pool, 8)
            hm = head_mask[:, :, :].rearrange("p h d -> p (h d)")
            nc.vector.tensor_scalar(neg_half_sum[:, :], hm, -0.5 / HEAD_DIM, None, ALU.mult).then_inc(c_dve, 1)
            nc.vector.tensor_copy(iota_e[:, :], iota_ei[:, :]).then_inc(c_dve, 1)
            nc.vector.tensor_copy(tok2_f[:, :], tok2_i[:, :]).then_inc(c_dve, 1)
            nc.vector.tensor_copy(region_f[:, :, :], region_i[:, :, :]).then_inc(c_dve, 1)
            nc.vector.tensor_copy(blk_f[:, :], blk_i[:, :]).then_inc(c_dve, 1)
            nc.vector.tensor_copy(blk_row_f[:, :, :], blk_row_i[:, :, :]).then_inc(c_dve, 1)
            nc.vector.tensor_copy(place[:, 0, GT, :], region_i[:, 0, :]).then_inc(c_dve, 1)
            nc.vector.tensor_copy(place[:, HALF_GROUPS + 1, GT, :], region_i[:, 1, :]).then_inc(c_dve, 1)
            nc.vector.tensor_copy(kv_den[:, 0, DIM:DIM + HEADS], head_mask[:, :, 0]).then_inc(c_dve, 1)
            nc.vector.tensor_copy(kv_den[:, 1, DIM:DIM + HEADS], head_mask[:, :, 0]).then_inc(c_dve, 1)
            dve.wait_ge(fold_in, 16)
            nc.vector.scalar_tensor_tensor(blk_r[:, :], r_s[:, :], float(HEAD_DIM) ** -0.5, hm,
                                           ALU.mult, ALU.mult).then_inc(c_dve, 1)
            dve.wait_ge(rest_in, 16)
            nc.vector.tensor_copy(bo_split[0:1, :, :], bc(bo_s[0:1, :], 1, [1, GT, DIM])).then_inc(c_dve, 1)
            dve.wait_ge(c_dve, 12)
            nc.vector.tensor_tensor(bo_rest[0:1, 0, :], bo_s[0:1, :], bo_split[0:1, 0, :],
                                    ALU.subtract).then_inc(c_dve, 1)
            dve.wait_ge(c_dve, 13)
            nc.vector.tensor_copy(bo_split[32:33, :, :], bc(bo_rest[0:1, 0, :], 1, [1, GT, DIM])).then_inc(c_dve, 1)
            dve.wait_ge(c_dve, 14)
            nc.vector.tensor_copy(bo_rest[32:33, 0, :], bo_rest[0:1, 0, :]).then_inc(c_dve, 1)
            dve.wait_ge(c_dve, 15)
            nc.vector.tensor_tensor(bo_rest[32:33, 1, :], bo_rest[32:33, 0, :], bo_split[32:33, 0, :],
                                    ALU.subtract).then_inc(c_dve, 1)
            dve.wait_ge(c_dve, 16)
            nc.vector.tensor_copy(bo_split[64:65, :, :], bc(bo_rest[32:33, 1, :], 1, [1, GT, DIM])).then_inc(c_dve, 1)

            grouped = [P, GT, HEADS, HEAD_DIM]

            def turn(i, h, par):
                a, b, c, d = i, i - 1, i - 2, i - 3
                if live(c):
                    dve.wait_ge(pe_wo, c + 1)
                    if isinstance(c, int) and c < 3:
                        dve.wait_ge(x_in_a, 16 * 3)
                    else:
                        dve.wait_ge(x_in_b, 16 * (GROUPS - 3))
                    nc.vector.tensor_tensor(resid[:, :, :], B[5][:, :].rearrange("p (t d) -> p t d", t=GT),
                                            x_all[:, bass.ds(c * GT, GT), :], ALU.add).then_inc(dv_res, 1)
                    dve.wait_ge(dv_res, c + 1)
                    for t in range(GT):
                        st = nc.vector.bn_stats(stats[:, t, :], resid[:, t, :])
                    st.then_inc(dv_stat, 1)
                    constants_stand(dve)
                    dve.wait_ge(dv_stat, c + 1)
                    for t in range(GT):
                        st = nc.vector.bn_aggr(meanvar[:, t, :], stats[:, t, :])
                    st.then_inc(dv_mv, 1)
                    dve.wait_ge(dv_mv, c + 1)
                    nc.vector.tensor_scalar(var_eps[:, :], meanvar[:, :, 1], 4.0, 4.0 * LN_EPS,
                                            ALU.mult, ALU.add).then_inc(dv_eps, 1)
                if live(d):
                    dve.wait_ge(pe_place, d + 1)
                    nc.vector.tensor_tensor(
                        place[:, bass.ds(d + h + 1, 1), :, :].rearrange("p a t e -> p (a t) e"),
                        B[7][:, 64:64 + (GT + 1) * EXPERTS].rearrange("p (t e) -> p t e", e=EXPERTS),
                        place[:, bass.ds(d + h, 1), GT, :].to_broadcast([P, GT + 1, EXPERTS]),
                        ALU.add).then_inc(dv_place, 1)
                    dve.wait_ge(dv_place, d + 1)
                    nc.vector.tensor_tensor(
                        picked[:, :, :, :], chosen[:, :, :, :],
                        place[:, bass.ds(d + h + 1, 1), 0:GT, :].to_broadcast([P, TOP_K, GT, EXPERTS]),
                        ALU.mult).then_inc(dv_pick, 1)
                    dve.wait_ge(dv_pick, d + 1)
                    with nc.allow_low_precision(reason="row numbers are whole and below 2**24"):
                        nc.vector.tensor_reduce(
                            slots[:, 1 - par, :, :].rearrange("p t k -> p k t"),
                            picked[:, :, :, :], AX_X, ALU.add).then_inc(dv_slot, 1)
                if live(c):
                    dve.wait_ge(pl_rstd, c + 1)
                    nc.vector.scalar_tensor_tensor(shift[:, :], meanvar[:, :, 0], -1.0, rstd[:, :],
                                                   ALU.mult, ALU.mult).then_inc(dv_shift, 1)
                if live(b):
                    dve.wait_ge(pe_kv, b + 1)
                    nc.vector.tensor_tensor(
                        kv_den[:, :, 0:DIM], B[3][:, 0:2 * DIM].rearrange("p (a d) -> p a d", a=2),
                        bc(hm, 1, [P, 2, DIM]), ALU.mult).then_inc(dv_kv, 1)
                if live(a):
                    dve.wait_ge(pe_v, a + 1)
                    nc.vector.tensor_tensor(v_tok[:, :, :], B[0][:, :].rearrange("p (t d) -> p t d", t=GT),
                                            bc(bv_s[:, :], 1, [P, GT, DIM]), ALU.add).then_inc(dv_v, 1)
                if live(b):
                    dve.wait_ge(pe_att, b + 1)
                    att = [B[4 + m][:, 0:2 * (DIM + HEADS)].rearrange("p (t d) -> p t d", t=2) for m in range(2)]
                    for m in range(2):
                        st = nc.vector.tensor_scalar(den[:, 2 * m:2 * m + 2, :], att[m][:, :, DIM:DIM + HEADS],
                                                     1e-8, None, ALU.add)
                    st.then_inc(dv_den, 1)
                    dve.wait_ge(dv_den, b + 1)
                    nc.vector.reciprocal(zrec[:, :, :], den[:, :, :]).then_inc(dv_z, 1)
                    dve.wait_ge(dv_z, b + 1)
                    for m in range(2):
                        st = nc.vector.tensor_tensor(
                            attn[:, 2 * m:2 * m + 2, :].rearrange("p t (h e) -> p t h e", h=HEADS),
                            att[m][:, :, 0:DIM].rearrange("p t (h e) -> p t h e", h=HEADS),
                            bc(zrec[:, 2 * m:2 * m + 2, :], 3, [P, 2, HEADS, HEAD_DIM]), ALU.mult)
                    st.then_inc(dv_att, 1)
                if live(c):
                    constants_stand(dve)
                    dve.wait_ge(pe_logit, c + 1)
                    for t in range(GT):
                        st = nc.vector.max(top8[:, t, :], B[7][:, t * EXPERTS:(t + 1) * EXPERTS])
                    st.then_inc(dv_top, 1)
                    constants_stand(dve)
                    dve.wait_ge(dv_top, c + 1)
                    for t in range(GT):
                        st = nc.vector.max_index(idx8[:, t, :], top8[:, t, :], B[7][:, t * EXPERTS:(t + 1) * EXPERTS])
                    st.then_inc(dv_idx, 1)
                    nc.vector.tensor_tensor(gap8[:, :, :], top8[:, :, :], top8[:, :, 0:1].to_broadcast([P, GT, 8]),
                                            ALU.subtract).then_inc(dv_gap, 1)
                    dve.wait_ge(dv_idx, c + 1)
                    nc.vector.tensor_tensor(
                        chosen[:, :, :, :],
                        bc(idx8[:, :, 0:TOP_K].rearrange("p t k -> p k t"), 3, [P, TOP_K, GT, EXPERTS]),
                        iota_e[:, :].unsqueeze(1).unsqueeze(1).to_broadcast([P, TOP_K, GT, EXPERTS]),
                        ALU.is_equal).then_inc(dv_cho, 1)
                    dve.wait_ge(dv_cho, c + 1)
                    nc.vector.tensor_tensor(either[:, :, :], chosen[:, 0, :, :], chosen[:, 1, :, :],
                                            ALU.add).then_inc(dv_both, 1)
                    dve.wait_ge(ac_exp8, c + 1)
                    nc.vector.tensor_reduce(sum8[:, :], exp8[:, :, :], AX_X, ALU.add).then_inc(dv_sum, 1)
                    dve.wait_ge(dv_sum, c + 1)
                    nc.vector.tensor_scalar(wden[:, :], sum8[:, :], 1e-6, 1.0, ALU.mult, ALU.add).then_inc(dv_wd, 1)
                    dve.wait_ge(dv_wd, c + 1)
                    nc.vector.tensor_tensor(wden2[:, :], wden[:, :], exp8[:, :, 1], ALU.add).then_inc(dv_wd2, 1)
                    pay = rows_now[:, par, :, :]
                    nc.vector.tensor_copy(pay[:, :, DIM:DIM + 1], tok2_f[:, bass.ds(c * GT, GT)].unsqueeze(2))
                    nc.vector.tensor_copy(pay[:, :, DIM + 1:DIM + 2], idx8[:, :, 1:2])
                    dve.wait_ge(dv_wd2, c + 1)
                    nc.vector.reciprocal(pay[:, :, DIM + 2:DIM + 3], wden2[:, :].unsqueeze(2)).then_inc(dv_w1, 1)
                    dve.wait_ge(dv_w1, c + 1)
                    nc.vector.scalar_tensor_tensor(pay[:, :, DIM + 3:DIM + 4], exp8[:, :, 1:2], -1.0,
                                                   pay[:, :, DIM + 2:DIM + 3], ALU.add, ALU.mult).then_inc(dv_pay, 1)
                if isinstance(d, int) and d > 0 and d % HALF_GROUPS == HALF_GROUPS - 1:
                    table(h)
                if isinstance(i, int) and 0 <= i < 4:
                    for e in range(i * EXPERTS // 4, (i + 1) * EXPERTS // 4):
                        dve.wait_ge(w13_h, e + 1)
                        nc.vector.scalar_tensor_tensor(w13_lo[:, e, :], w13_s[:, e, :], 2.0,
                                                       w13_hi[:, e, :].bitcast(F32),
                                                       ALU.mult, ALU.subtract).then_inc(w13_l, 1)

            def table(h):
                n = 9 * h
                ends = place[:, (h + 1) * (HALF_GROUPS + 1) - 1, GT, :]
                nc.vector.tensor_copy(fill_at[:, h, :], ends).then_inc(fill_ready, 1)
                nc.vector.tensor_tensor(count_f[:, :], ends, region_f[:, h, :], ALU.subtract).then_inc(tb, 1)
                dve.wait_ge(tb, n + 1)
                nc.vector.tensor_scalar(count_i[:, :], count_f[:, :], float(P - 1), None, ALU.add).then_inc(tb, 1)
                dve.wait_ge(tb, n + 2)
                nc.vector.tensor_scalar(nblk_i[:, :], count_i[:, :], P.bit_length() - 1, None,
                                        ALU.arith_shift_right).then_inc(tb, 1)
                dve.wait_ge(tb, n + 3)
                nc.vector.tensor_copy(nblk_f[:, :], nblk_i[:, :]).then_inc(tb, 1)
                dve.wait_ge(tb, n + 4)
                nc.vector.tensor_tensor_scan(end_f[:, :], ones8[:, :], nblk_f[:, :], 0.0,
                                             ALU.mult, ALU.add).then_inc(tb, 1)
                nc.vector.tensor_scalar(skip_f[:, :], nblk_f[:, :], -float(P), float(REGION),
                                        ALU.mult, ALU.add).then_inc(tb, 1)
                dve.wait_ge(tb, n + 6)
                shape = [P, BLOCKS, EXPERTS]
                nc.vector.tensor_tensor(past[:, :, :], bc(end_f[:, :], 1, shape), bc(blk_f[:, :], 2, shape),
                                        ALU.is_le).then_inc(tb, 1)
                dve.wait_ge(tb, n + 7)
                nc.vector.tensor_tensor(past_skip[:, :, :], past[:, :, :], bc(skip_f[:, :], 1, shape),
                                        ALU.mult).then_inc(tb, 1)
                mine = slice(h * BLOCKS, (h + 1) * BLOCKS)
                nc.vector.tensor_reduce(blk_expert[:, mine], past[:, :, :], AX_X, ALU.add)
                dve.wait_ge(tb, n + 8)
                nc.vector.tensor_reduce(blk_skip[:, :], past_skip[:, :, :], AX_X, ALU.add).then_inc(tb, 1)
                dve.wait_ge(tb, n + 9)
                nc.vector.tensor_scalar(blk_expert_i[:, LEAD + h * BLOCKS:LEAD + (h + 1) * BLOCKS], blk_expert[:, mine], float(EXPERTS - 1), None, ALU.min)
                nc.vector.tensor_tensor(blk_row[:, mine], blk_skip[:, :], blk_row_f[:, h, :],
                                        ALU.add).then_inc(table_ready, 1)

            stage_a_turns(dve, turn)

            def xT_copy(j, u):
                dve.wait_ge(d_xTh, j + 1)
                nc.vector.tensor_tensor(blk_xT_lo[:, u % 2, :], B[4 + u % 2][:, 0:P],
                                        blk_xT_hi[:, u % 2, :].bitcast(F32), ALU.subtract).then_inc(d_xTc, 1)

            def gate_up(j, u):
                dve.wait_ge(d_silu, j + 1)
                nc.vector.tensor_tensor(hidden[:, u % 2, :], silu_g[:, u % 2, :], B[u % 2][:, INNER:2 * INNER],
                                        ALU.mult).then_inc(d_mul, 1)

            def weigh(j, u, again):
                dve.wait_ge(d_y, j + 1)
                if again is not None:
                    dve.wait_ge(blk_stored[u], again)
                nc.vector.scalar_tensor_tensor(blk_out[:, u, :], B[6 + u % 2][:, 0:DIM], blk_w[:, u:u + 1],
                                               blk_in[:, u, 0:DIM], ALU.mult, ALU.add).then_inc(d_yw, 1)

            def payload(i, part, start):
                s = slice(part * UNROLL // 2, (part + 1) * UNROLL // 2)
                for u in range(s.start, s.stop):
                    dve.wait_ge(blk_loaded[u], 16 * (i + 1))
                    if not start:
                        dve.wait_ge(blk_stored[u], 16 * i)
                nc.vector.tensor_tensor(is_second[:, s], blk_in[:, s, DIM + 1],
                                        blk_expert[:, bass.ds(i * UNROLL + s.start, UNROLL // 2)],
                                        ALU.is_equal).then_inc(d_chain, 1)
                dve.wait_ge(d_chain, (i * 2 + part) * 2 + 1)
                nc.vector.tensor_tensor(w_diff[:, s], is_second[:, s], blk_in[:, s, DIM + 3],
                                        ALU.mult).then_inc(d_chain, 1)
                nc.vector.tensor_tensor(blk_dst[:, s], is_second[:, s], blk_in[:, s, DIM], ALU.add)
                dve.wait_ge(d_chain, (i * 2 + part) * 2 + 2)
                nc.vector.tensor_tensor(blk_w[:, s], w_diff[:, s], blk_in[:, s, DIM + 2],
                                        ALU.add).then_inc(d_pay, 1)

            def pair_sum(j, m):
                g = 2 * m + j
                dve.wait_ge(pair_loaded[j], 16 * (m + 1))
                if not (isinstance(m, int) and m == 0):
                    dve.wait_ge(f_fin, g - 1)
                pr = pair_in[:, j, :, :, :].rearrange("p h t (k d) -> p (h t) k d", k=TOP_K)
                nc.vector.tensor_tensor(total[:, j, :, :], pr[:, :, 0, :], pr[:, :, 1, :], ALU.add).then_inc(f_add, 1)

            def pair_stats(j, m):
                dve.wait_ge(f_add, 2 * m + j + 1)
                for t in range(GT):
                    st = nc.vector.bn_stats(stats2[:, j, t, :], total[:, j, t, :])
                st.then_inc(f_stat, 1)

            def pair_var(j, m):
                g = 2 * m + j
                constants_stand(dve)
                dve.wait_ge(f_stat, g + 1)
                for t in range(GT):
                    st = nc.vector.bn_aggr(meanvar2[:, j, t, :], stats2[:, j, t, :])
                st.then_inc(f_mv, 1)
                dve.wait_ge(f_mv, g + 1)
                nc.vector.tensor_scalar(var_eps2[:, j, :], meanvar2[:, j, :, 1], LN_EPS, None,
                                        ALU.add).then_inc(f_eps, 1)

            def pair_shift(j, m):
                dve.wait_ge(f_rstd, 2 * m + j + 1)
                nc.vector.scalar_tensor_tensor(shift2[:, j, :], meanvar2[:, j, :, 0], -1.0, rstd2[:, j, :],
                                               ALU.mult, ALU.mult).then_inc(f_shift, 1)

            steps_of_turn = {1: (pair_sum, 0), 2: (pair_stats, 0), 3: (pair_var, 0), 4: (pair_sum, 1),
                             5: (pair_stats, 1), 6: (pair_var, 1), 8: (pair_shift, 0), 10: (pair_shift, 1)}

            def expert_turn(i, start, end, m=None):
                if start:
                    xT_copy(0, 0)
                    xT_copy(1, 1)
                for u in range(UNROLL):
                    j = i * UNROLL + u
                    if not (start and u < 2):
                        su = (u - 2) % UNROLL
                        again = None if (start or (u < 2 and isinstance(i, int) and i == 1)) else \
                            (16 * i if u >= 2 else 16 * (i - 1))
                        if su == 0:
                            dve.wait_ge(d_pay, 2 * i + 1)
                        elif su == UNROLL // 2:
                            dve.wait_ge(d_pay, 2 * i + 2)
                        weigh(j - 2, su, again)
                    gate_up(j, u)
                    if not (end and u >= UNROLL - 2):
                        xT_copy(j + 2, u)
                    if u == 1:
                        payload(i, 0, start)
                    if u == 1 + UNROLL // 2:
                        payload(i, 1, start)
                    if m is not None and u in steps_of_turn:
                        step, which = steps_of_turn[u]
                        step(which, m)

            expert_turn(0, True, False)
            expert_turn(1, False, False)
            with dve.Fori(2, FIRST_PAIRS) as i:
                expert_turn(i, False, False)
            expert_turn(FIRST_PAIRS, False, False, 0)
            with dve.Fori(1, HALF_PAIRS) as m:
                expert_turn(m + FIRST_PAIRS, False, False, m)
            expert_turn(TURNS - 1, False, True)
            weigh(TURNS * UNROLL - 2, UNROLL - 2, 16 * (TURNS - 1))
            weigh(TURNS * UNROLL - 1, UNROLL - 1, 16 * (TURNS - 1))

            def pair_turn(m, start):
                pair_sum(0, m)
                pair_stats(0, m)
                if not start:
                    pair_shift(1, m - 1)
                pair_var(0, m)
                pair_sum(1, m)
                pair_stats(1, m)
                pair_shift(0, m)
                pair_var(1, m)

            pair_turn(HALF_PAIRS, True)
            with dve.Fori(HALF_PAIRS + 1, 2 * HALF_PAIRS) as m:
                pair_turn(m, False)
            pair_shift(1, 2 * HALF_PAIRS - 1)

        @block.tensor
        def _(pe):
            pe.wait_ge(c_dve, 11)
            nc.tensor.matmul(B[0][:, 0:P], wq_s[:, :], blk_r[:, :], start=True, stop=True)
            nc.tensor.matmul(B[0][:, P:P + 1], blk_r[:, :], bq_s[:, :], start=True, stop=True).then_inc(c_pe, 1)
            nc.tensor.matmul(B[1][:, 0:P], wk_s[:, :], blk_r[:, :], start=True, stop=True)
            nc.tensor.matmul(B[1][:, P:P + 1], blk_r[:, :], bk_s[:, :], start=True, stop=True).then_inc(c_pe, 1)
            pe.wait_ge(c_act, 5)
            pe.wait_ge(c_dve, 17)

            def turn(i, h, par):
                n, a, b, c, d = i + 1, i, i - 1, i - 2, i - 3
                if live(a):
                    pe.wait_ge(ac_xT, a + 1)
                    if not first(a):
                        pe.wait_ge(ac_fq, a)
                    nc.tensor.matmul(B[1][:, :], wqT_s[:, :], xT[:, :], start=True, stop=True).then_inc(pe_q, 1)
                if live(b):
                    pe.wait_ge(ac_fk, b + 1)
                    if not first(b):
                        pe.wait_ge(dv_kv, b)
                    for t in range(GT):
                        mm = nc.tensor.transpose(B[3][:, t * P:(t + 1) * P], k_feat[:, t * P:(t + 1) * P], ident[:, :])
                    mm.then_inc(pe_kT, 1)
                if live(d):
                    pe.wait_ge(dv_both, d + 1)
                    at = 64
                    nc.tensor.matmul(B[7][:, at:at + GT * EXPERTS], before[:, :],
                                     either[:, :, :].rearrange("p t e -> p (t e)"), start=True, stop=False,
                                     skip_group_check=True)
                    for t in range(GT):
                        lo = (t + 1) * EXPERTS
                        mm = nc.tensor.matmul(B[7][:, at + lo:at + (GT + 1) * EXPERTS], ones_b[:, :],
                                              either[:, 0:GT - t, :].rearrange("p t e -> p (t e)"),
                                              start=False, stop=(t == GT - 1), skip_group_check=True)
                    mm.then_inc(pe_place, 1)
                if live(a):
                    if not first(a):
                        pe.wait_ge(ac_fk, a)
                    nc.tensor.matmul(B[2][:, :], wkT_s[:, :], xT[:, :], start=True, stop=True).then_inc(pe_k, 1)
                if live(b):
                    pe.wait_ge(ac_kT, b + 1)
                    pe.wait_ge(dv_v, b + 1)
                    for m in range(2):
                        for t in range(2):
                            mm = nc.tensor.matmul(B[3][:, m * DIM:(m + 1) * DIM], k_tok[:, 2 * m + t, :],
                                                  v_tok[:, 2 * m + t, :], start=(t == 0), stop=(t == 1))
                    mm.then_inc(pe_kv, 1)
                if live(a):
                    pe.wait_ge(ac_q2, a + 1)
                    nc.tensor.matmul(B[1][:, :], wqrT[:, :], xT[:, :], start=True, stop=False)
                    nc.tensor.matmul(B[1][:, :], neg_half_sum[:, :], q_sq[:, :], start=False, stop=True).then_inc(pe_fq, 1)
                    for t in range(GT):
                        mm = nc.tensor.matmul(B[0][:, t * P:(t + 1) * P], xT[:, t * P:(t + 1) * P], wvT_s[:, :],
                                              start=True, stop=True)
                    mm.then_inc(pe_v, 1)
                if live(b):
                    pe.wait_ge(ac_fq, b + 1)
                    pe.wait_ge(dv_kv, b + 1)
                    if not first(b):
                        pe.wait_ge(ac_attT, b)
                        pe.wait_ge(dv_res, b)
                    for t in range(GT):
                        mm = nc.tensor.matmul(B[4 + t // 2][:, (t % 2) * (DIM + HEADS):(t % 2 + 1) * (DIM + HEADS)],
                                              q_feat[:, t * P:(t + 1) * P], kv_den[:, t // 2, :], start=True, stop=True)
                    mm.then_inc(pe_att, 1)
                if live(c):
                    pe.wait_ge(ac_rows, c + 1)
                    if not first(c):
                        pe.wait_ge(ac_x2T, c)
                    for t in range(GT):
                        mm = nc.tensor.transpose(B[6][:, t * P:(t + 1) * P], rows_now[:, par, t, 0:DIM], ident[:, :])
                    mm.then_inc(pe_x2T, 1)
                if live(a):
                    pe.wait_ge(ac_k2, a + 1)
                    nc.tensor.matmul(B[2][:, :], wkrT[:, :], xT[:, :], start=True, stop=False)
                    nc.tensor.matmul(B[2][:, :], neg_half_sum[:, :], k_sq[:, :], start=False, stop=True).then_inc(pe_fk, 1)
                if live(b):
                    pe.wait_ge(dv_att, b + 1)
                    for t in range(GT):
                        mm = nc.tensor.transpose(B[4][:, t * P:(t + 1) * P], attn[:, t, :], ident[:, :])
                    mm.then_inc(pe_attT, 1)
                if live(n):
                    pe.wait_ge(xg_in, 16 * (n + 1))
                    if live(a):
                        pe.wait_ge(dv_v, a + 1)
                    for t in range(GT):
                        mm = nc.tensor.transpose(B[0][:, t * P:(t + 1) * P], x_in[:, t, :], ident[:, :])
                    mm.then_inc(pe_xT, 1)
                if live(c):
                    pe.wait_ge(ac_x2T, c + 1)
                    if not first(c):
                        pe.wait_ge(dv_both, c)
                    for t in range(GT):
                        mm = nc.tensor.matmul(B[7][:, t * EXPERTS:(t + 1) * EXPERTS], x2T[:, t, :], router_s[:, :],
                                              start=True, stop=True)
                    mm.then_inc(pe_logit, 1)
                if live(b):
                    pe.wait_ge(ac_attT, b + 1)
                    nc.tensor.matmul(B[5][:, :], ones_b[:, :], bo_split[:, :, :].rearrange("p t d -> p (t d)"),
                                     start=True, stop=False)
                    for t in range(GT):
                        mm = nc.tensor.matmul(B[5][:, t * P:(t + 1) * P], attnT[:, t, :], woT_s[:, :],
                                              start=False, stop=(t == GT - 1))
                    mm.then_inc(pe_wo, 1)

            stage_a_turns(pe, turn)

            def experts_of(lo, count):
                return nc.values_load_multi_w_load_instructions(
                    blk_expert_i[0:1, bass.ds(lo + LEAD, count)], (mybir.EngineType.PE,),
                    min_val=0, max_val=EXPERTS - 1,
                    skip_runtime_bounds_check_because="the table holds a count of experts, at most the last")[1]

            def xT_blk(i, u, start):
                j = i * UNROLL + u
                pe.wait_ge(blk_loaded[u], 16 * (i + 1))
                if not start:
                    pe.wait_ge(d_xTc, j - 1)
                nc.tensor.transpose(B[4 + u % 2][:, 0:P], blk_in[:, u, 0:DIM], ident[:, :]).then_inc(d_xT, 1)

            def up(j, u, e, start):
                pe.wait_ge(d_xTc, j + 1)
                if not start:
                    pe.wait_ge(d_mul, j - 1)
                parts = [(blk_xT_hi, w13_hi), (blk_xT_hi, w13_lo), (blk_xT_lo, w13_hi)]
                for n, (rows, weights) in enumerate(parts):
                    mm = nc.tensor.matmul(B[u % 2][:, :], rows[:, u % 2, :],
                                          weights[:, bass.ds(e, 1), :].rearrange("p a i -> p (a i)"),
                                          start=(n == 0), stop=(n == 2))
                mm.then_inc(d_h, 1)

            def hidT(j, u, start):
                pe.wait_ge(d_mul, j + 1)
                if not start:
                    pe.wait_ge(d_hTc, j - 1)
                for c in range(2):
                    mm = nc.tensor.transpose(B[2 + u % 2][:, c * P:(c + 1) * P], hidden[:, u % 2, c * P:(c + 1) * P],
                                             ident[:, :])
                mm.then_inc(d_hT, 1)

            def down(j, u, e, start):
                pe.wait_ge(d_hTc, j + 1)
                if not start:
                    pe.wait_ge(d_yw, j - 1)
                for c in range(2):
                    mm = nc.tensor.matmul(B[6 + u % 2][:, 0:DIM], hiddenT[:, u % 2, c * P:(c + 1) * P],
                                          w2_s[:, bass.ds(e, 1), c, :].rearrange("p a d -> p (a d)"),
                                          start=(c == 0), stop=(c == 1))
                mm.then_inc(d_y, 1)

            def expert_turn(i, start, end):
                if start:
                    es = dict(zip(range(UNROLL), experts_of(0, UNROLL)))
                    xT_blk(0, 0, True)
                    xT_blk(0, 1, True)
                else:
                    es = dict(zip(range(-LEAD, UNROLL), experts_of(i * UNROLL - LEAD, LEAD + UNROLL)))
                for u in range(UNROLL):
                    j = i * UNROLL + u
                    up(j, u, es[u], start and u < 2)
                    if not (start and u < 2):
                        down(j - 2, u, es[u - 2], start and u < 4)
                    if u < UNROLL - 2:
                        xT_blk(i, u + 2, False)
                    elif not end:
                        xT_blk(i + 1, u + 2 - UNROLL, False)
                    if not (start and u == 0):
                        hidT(j - 1, u + 1, start and u < 3)

            pe.wait_ge(w13_l, EXPERTS)
            pe.wait_ge(w2_in, 16)
            pe.wait_ge(table_ready, 1)
            expert_turn(0, True, False)
            with pe.Fori(1, TURNS // 2) as i:
                expert_turn(i, False, False)
            pe.wait_ge(table_ready, 2)
            with pe.Fori(TURNS // 2, TURNS - 1) as i:
                expert_turn(i, False, False)
            expert_turn(TURNS - 1, False, True)
            last = TURNS * UNROLL - 1
            el = experts_of(last - 3, 4)[2:]
            down(last - 1, 0, el[0], False)
            hidT(last, 1, False)
            down(last, 1, el[1], False)


def kernel(**inputs):
    import numpy as _np
    import concourse.bacc as _bacc
    from concourse import mybir as _mybir
    from concourse.bass_utils import run_bass_kernel_spmd as _run

    get = {k: _np.asarray(v) for k, v in inputs.items()}
    wq, wk, wv, wo = (get["L0_attn_W" + c] for c in "qkvo")
    bq, bk, bv, bo = (get["L0_attn_b" + c] for c in "qkvo")
    h, e = HEADS, HEAD_DIM
    laid = {
        "x": get["L0_attn_x"],
        "weights_fold": _np.concatenate(
            [_np.broadcast_to(get["L0_attn_R"][None, :, None, :], (h, e, h, e)).reshape(P, P), wq, wk,
             bq.reshape(P, 1), bk.reshape(P, 1)], axis=1),
        "weights_rest": _np.concatenate(
            [wq.T, wk.T, wv.T, wo.T, _np.broadcast_to(bv, (P, DIM)), _np.broadcast_to(bo, (P, DIM)),
             get["L0_ffn_router_w"].T], axis=1),
        "w13": get["L0_ffn_w13"].transpose(1, 0, 2),
        "w2": get["L0_ffn_w2"].reshape(EXPERTS, 2, P, DIM).transpose(2, 0, 1, 3),
    }
    nc = _bacc.Bacc("TRN2", target_bir_lowering=False, num_devices=1)
    arrays, args = {}, []
    for name, a in laid.items():
        a = _np.ascontiguousarray(a)
        arrays[f"in_{name}"] = a
        args.append(nc.dram_tensor(f"in_{name}", a.shape, _mybir.dt.from_np(a.dtype), kind="ExternalInput").ap())
    args.append(nc.dram_tensor("out_0", (BATCHES, SEQ, DIM), _mybir.dt.float32, kind="ExternalOutput").ap())
    moe_kernel(nc, *args)
    r = _run(nc, [arrays], core_ids=[0])
    return r.results[0]["out_0"]
```

```python
from contextlib import ExitStack

import numpy as np

import concourse.bass as bass
from concourse import mybir

ALU = mybir.AluOpType
ACT = mybir.ActivationFunctionType
F32 = mybir.dt.float32
F32R = mybir.dt.float32r
BF16 = mybir.dt.bfloat16
U32 = mybir.dt.uint32
I32 = mybir.dt.int32
AX_X = mybir.AxisListType.X

P = 128
DIM = 128
HEADS = 16
HEAD_DIM = DIM // HEADS
BATCHES, SEQ = 32, 256
TOKENS = BATCHES * SEQ
EXPERTS = 8
INNER = 256
TOP_K = 2
LN_EPS = 1e-5

GT = 4
GROUPS = TOKENS // (GT * P)
TILES = TOKENS // P
HALVES = 2
HALF_GROUPS = GROUPS // HALVES
CONSTANTS = 10
PAYLOAD = 4
ROW = DIM + PAYLOAD
CHOICES = TOP_K * TOKENS
HALF_CHOICES = CHOICES // HALVES
UNROLL = 12
BLOCKS = -(-(HALF_CHOICES // P + EXPERTS - 1) // UNROLL) * UNROLL
REGION = TOKENS // HALVES + P
HALF_ROWS = EXPERTS * REGION + UNROLL * P
FILLS = HALVES * (EXPERTS + UNROLL)
TURNS = HALVES * BLOCKS // UNROLL
LEAD = 4
Q, K, QR, KR = range(4)
HALF_PAIRS = HALF_GROUPS // 2
QUADS = HALF_GROUPS // 4
FIRST_PAIRS = TURNS // 2 + 1


def moe_kernel(nc, x, weights_fold, weights_rest, w13, w2, out):
    with ExitStack() as ctx:
        def sb(name, shape, dt=F32):
            return ctx.enter_context(nc.sbuf_tensor(name, shape, dt))

        def bank(name, shape, dt=F32):
            return ctx.enter_context(nc.psum_tensor(name, shape, dt))

        def sem(name):
            return ctx.enter_context(nc.semaphore(name))

        sorted_rows = nc.dram_tensor("sorted_rows", [HALVES * HALF_ROWS, ROW], F32, kind="Internal").ap()
        expert_out = nc.dram_tensor("expert_out", [CHOICES + FILLS * P, DIM], F32, kind="Internal").ap()

        fold_s = sb("fold_s", [P, 3 * DIM + 2])
        r_s, wq_s, wk_s = (fold_s[:, n * DIM:(n + 1) * DIM] for n in range(3))
        bq_s, bk_s = fold_s[:, 3 * DIM:3 * DIM + 1], fold_s[:, 3 * DIM + 1:3 * DIM + 2]
        rest_s = sb("rest_s", [P, 6 * DIM + EXPERTS])
        wvT_s, woT_s, bv_s, bo_s = (rest_s[:, n * DIM:(n + 1) * DIM] for n in range(2, 6))
        router_in = rest_s[:, 6 * DIM:6 * DIM + EXPERTS]
        router_s = sb("router_s", [P, EXPERTS])
        w13_s = sb("w13_s", [P, EXPERTS, 2 * INNER])
        w13_hi = sb("w13_hi", [P, EXPERTS, 2 * INNER], F32R)
        w13_lo = sb("w13_lo", [P, EXPERTS, 2 * INNER], F32R)
        w2_s = sb("w2_s", [P, EXPERTS, 2, DIM])
        ident = sb("ident", [P, P])
        head_mask = sb("head_mask", [P, HEADS, HEAD_DIM])
        neg_half_sum = sb("neg_half_sum", [P, P], F32R)
        blk_r = sb("blk_r", [P, P])
        proj_hi = sb("proj_hi", [P, 4, DIM], F32R)
        proj_lo = sb("proj_lo", [P, 4, DIM], F32R)
        bqr, bkr = sb("bqr", [P, 1]), sb("bkr", [P, 1])
        before = sb("before", [P, P], BF16)
        ones_b = sb("ones_b", [P, P], BF16)
        bo_split = sb("bo_split", [P, GT, DIM], BF16)
        bo_rest = sb("bo_rest", [P, 2, DIM])
        iota_e = sb("iota_e", [P, EXPERTS], U32)
        iota_ei = sb("iota_ei", [P, EXPERTS], I32)
        minus_half = sb("minus_half", [P, GT])
        tok2_i = sb("tok2_i", [P, TILES], I32)
        fill_i = sb("fill_i", [P, FILLS], I32)
        fill_rows = sb("fill_rows", [P, FILLS, ROW])
        region_i = sb("region_i", [P, HALVES, EXPERTS], I32)
        region_f = sb("region_f", [P, HALVES, EXPERTS])
        blk_i = sb("blk_i", [P, BLOCKS], I32)
        blk_f = sb("blk_f", [P, BLOCKS])
        blk_row_i = sb("blk_row_i", [P, HALVES, BLOCKS], I32)
        blk_row_f = sb("blk_row_f", [P, HALVES, BLOCKS])
        ones8 = sb("ones8", [P, EXPERTS])

        x_all = sb("x_all", [P, TILES, DIM])
        x_in = sb("x_in", [P, GT, DIM])
        xT = sb("xT", [P, 2, GT * P])
        xT_hi = sb("xT_hi", [P, 2, GT * P], F32R)
        xT_lo = sb("xT_lo", [P, 2, GT * P], F32R)
        q_sq, k_sq = sb("q_sq", [P, GT * P]), sb("k_sq", [P, GT * P])
        q_sq_hi, k_sq_hi = sb("q_sq_hi", [P, GT * P], F32R), sb("k_sq_hi", [P, GT * P], F32R)
        q_sq_lo, k_sq_lo = sb("q_sq_lo", [P, GT * P], F32R), sb("k_sq_lo", [P, GT * P], F32R)
        q_feat, k_feat = sb("q_feat", [P, GT * P]), sb("k_feat", [P, GT * P])
        k_tok = sb("k_tok", [P, GT, DIM])
        v_tok = sb("v_tok", [P, GT, DIM])
        kv_den = sb("kv_den", [P, 2, DIM + HEADS])
        den = sb("den", [P, GT, HEADS])
        zrec = sb("zrec", [P, GT, HEADS])
        attn = sb("attn", [P, GT, DIM])
        attnT = sb("attnT", [P, GT, P])
        resid = sb("resid", [P, GT, DIM])
        stats = sb("stats", [P, GT, 6])
        meanvar = sb("meanvar", [P, GT, 2])
        var_eps = sb("var_eps", [P, GT])
        rstd = sb("rstd", [P, GT])
        shift = sb("shift", [P, GT])
        x2T = sb("x2T", [P, GT, P])
        rows_now = sb("rows_now", [P, 2, GT, ROW])
        tok2_f = sb("tok2_f", [P, TILES])
        top8 = sb("top8", [P, GT, 8])
        idx8 = sb("idx8", [P, GT, 8], U32)
        gap8 = sb("gap8", [P, GT, 8])
        exp8 = sb("exp8", [P, GT, 8])
        sum8 = sb("sum8", [P, GT])
        wden = sb("wden", [P, GT])
        wden2 = sb("wden2", [P, GT])
        chosen = sb("chosen", [P, TOP_K, GT, EXPERTS], BF16)
        either = sb("either", [P, GT, EXPERTS], BF16)
        place = sb("place", [P, GROUPS + HALVES, GT + 1, EXPERTS])
        picked = sb("picked", [P, TOP_K, GT, EXPERTS])
        slots = sb("slots", [P, 2, GT, TOP_K], U32)

        fill_at = sb("fill_at", [P, HALVES, EXPERTS], I32)
        count_f = sb("count_f", [P, EXPERTS])
        count_i = sb("count_i", [P, EXPERTS], I32)
        nblk_i = sb("nblk_i", [P, EXPERTS], I32)
        nblk_f = sb("nblk_f", [P, EXPERTS])
        end_f = sb("end_f", [P, EXPERTS])
        skip_f = sb("skip_f", [P, EXPERTS])
        past = sb("past", [P, BLOCKS, EXPERTS])
        past_skip = sb("past_skip", [P, BLOCKS, EXPERTS])
        blk_skip = sb("blk_skip", [P, BLOCKS])
        blk_expert = sb("blk_expert", [P, HALVES * BLOCKS])
        blk_expert_i = sb("blk_expert_i", [P, LEAD + HALVES * BLOCKS], I32)
        blk_row = sb("blk_row", [P, HALVES * BLOCKS], I32)

        blk_in = sb("blk_in", [P, UNROLL, ROW])
        blk_xT_hi = sb("blk_xT_hi", [P, 2, P], F32R)
        blk_xT_lo = sb("blk_xT_lo", [P, 2, P], F32R)
        silu_g = sb("silu_g", [P, 2, INNER])
        hidden = sb("hidden", [P, 2, INNER])
        hiddenT = sb("hiddenT", [P, 2, INNER])
        blk_out = sb("blk_out", [P, UNROLL, DIM])
        is_second = sb("is_second", [P, UNROLL])
        w_diff = sb("w_diff", [P, UNROLL])
        blk_w = sb("blk_w", [P, UNROLL])
        blk_dst = sb("blk_dst", [P, UNROLL], U32)

        assert EXPERTS * 2 * INNER == 4 * GT * TOP_K * DIM

        def pair_in(b):
            return w13_s[:, 2 * b:2 * b + 2, :]

        stats2 = sb("stats2", [P, 4, GT, 6])
        meanvar2 = sb("meanvar2", [P, 4, GT, 2])
        var_eps2 = sb("var_eps2", [P, 4, GT])
        rstd2 = sb("rstd2", [P, 4, GT])
        shift2 = sb("shift2", [P, 4, GT])

        B = [bank(f"bank{n}", [P, 512]) for n in range(8)]

        fold_in, rest_in, xg_in = sem("fold_in"), sem("rest_in"), sem("xg_in")
        w13_in, w2_in, w13_h, w13_l = sem("w13_in"), sem("w2_in"), sem("w13_h"), sem("w13_l")
        x_in_a, x_in_b = sem("x_in_a"), sem("x_in_b")
        fill_rows_ready, dummy_out = sem("fill_rows_ready"), sem("dummy_out")
        scattered = [sem(f"scattered{par}") for par in range(2)]
        filled = [sem(f"filled{h}") for h in range(HALVES)]
        blk_loaded = [sem(f"blk_loaded{u}") for u in range(UNROLL)]
        blk_stored = [sem(f"blk_stored{u}") for u in range(UNROLL)]
        pair_loaded = [sem(f"pair_loaded{b}") for b in range(4)]
        out_stored = sem("out_stored")
        c_pool, c_dve, c_pe, c_act = sem("c_pool"), sem("c_dve"), sem("c_pe"), sem("c_act")
        pe_xT, pe_q, pe_k, pe_v, pe_fq, pe_fk = (sem(n) for n in ("pe_xT", "pe_q", "pe_k", "pe_v", "pe_fq", "pe_fk"))
        pe_kT, pe_kv, pe_att, pe_attT, pe_wo = (sem(n) for n in ("pe_kT", "pe_kv", "pe_att", "pe_attT", "pe_wo"))
        pe_x2T, pe_logit, pe_place = (sem(n) for n in ("pe_x2T", "pe_logit", "pe_place"))
        ac_xT, ac_q2, ac_k2, ac_fq, ac_fk, ac_kT = (sem(n) for n in ("ac_xT", "ac_q2", "ac_k2", "ac_fq", "ac_fk", "ac_kT"))
        ac_attT, ac_x2T, ac_rows, ac_exp8 = (sem(n) for n in ("ac_attT", "ac_x2T", "ac_rows", "ac_exp8"))
        dv_q2, dv_k2 = sem("dv_q2"), sem("dv_k2")
        ac_sq = sem("ac_sq")
        dv_xT, dv_v, dv_kv, dv_den, dv_z, dv_att = (sem(n) for n in ("dv_xT", "dv_v", "dv_kv", "dv_den", "dv_z", "dv_att"))
        dv_res, dv_stat, dv_mv, dv_eps, pl_rstd, dv_shift = (sem(n) for n in ("dv_res", "dv_stat", "dv_mv", "dv_eps", "pl_rstd", "dv_shift"))
        dv_top, dv_idx, dv_gap, dv_cho, dv_both = (sem(n) for n in ("dv_top", "dv_idx", "dv_gap", "dv_cho", "dv_both"))
        dv_sum, dv_wd, dv_wd2, dv_w1, dv_pay = (sem(n) for n in ("dv_sum", "dv_wd", "dv_wd2", "dv_w1", "dv_pay"))
        dv_place, dv_pick, dv_slot = (sem(n) for n in ("dv_place", "dv_pick", "dv_slot"))
        tb, fill_ready, table_ready = sem("tb"), sem("fill_ready"), sem("table_ready")
        d_xT, d_h, d_hT, d_y = (sem(n) for n in ("d_xT", "d_h", "d_hT", "d_y"))
        d_xTh, d_xTc, d_silu, d_mul, d_hTc, d_yw, d_pay, d_chain = (sem(n) for n in ("d_xTh", "d_xTc", "d_silu", "d_mul", "d_hTc", "d_yw", "d_pay", "d_chain"))
        f_add, f_stat, f_mv, f_eps, f_rstd, f_shift, f_fin = (sem(n) for n in ("f_add", "f_stat", "f_mv", "f_eps", "f_rstd", "f_shift", "f_fin"))

        x_tok = x.rearrange("(n h) (p t) d -> n p h t d", n=GROUPS, h=2, t=2)

        def x_group(n):
            return x_all[:, n * GT:(n + 1) * GT, :].rearrange("p (h t) d -> p h t d", h=2)

        def live(g):
            return not isinstance(g, int) or 0 <= g < GROUPS

        def first(g):
            return isinstance(g, int) and g == 0

        def bc(ap, axis, shape):
            return ap.unsqueeze(axis).to_broadcast(shape)

        def constants_stand(eng):
            eng.wait_ge(c_dve, CONSTANTS)

        def known(eng, value):
            return value if isinstance(value, int) else eng.compute_val(value)

        def stage_a_turns(eng, turn):
            def straight(lo, hi, h):
                for i in range(lo, hi):
                    turn(i, h, i % 2)

            def pairs(lo, hi, h):
                with eng.Fori(lo, hi, 2) as i:
                    turn(i, h, lo % 2)
                    turn(i + 1, h, (lo + 1) % 2)

            straight(-1, 4, 0)
            pairs(4, HALF_GROUPS + 2, 0)
            straight(HALF_GROUPS + 2, HALF_GROUPS + 3, 0)
            pairs(HALF_GROUPS + 3, GROUPS - 1, 1)
            straight(GROUPS - 1, GROUPS + 3, 1)

        block = ctx.enter_context(nc.Block())

        @block.sync
        def _(sp):
            x_in_v = x_in[:, :, :].rearrange("p (h t) d -> p h t d", h=2)
            sp.dma_start(x_in_v, x_tok[0]).then_inc(xg_in, 16)
            sp.dma_start(fold_s[:, :], weights_fold).then_inc(fold_in, 16)
            sp.dma_start(rest_s[:, :], weights_rest).then_inc(rest_in, 16)
            sp.dma_start(w13_s[:, :, :], w13).then_inc(w13_in, 16)
            sp.wait_ge(pe_xT, 1)
            sp.dma_start(x_in_v, x_tok[1]).then_inc(xg_in, 16)
            for n in range(0, 3):
                sp.dma_start(x_group(n), x_tok[n]).then_inc(x_in_a, 16)
            sp.wait_ge(pe_xT, 2)
            sp.dma_start(x_in_v, x_tok[2]).then_inc(xg_in, 16)
            for n in range(3, GROUPS):
                sp.dma_start(x_group(n), x_tok[n]).then_inc(x_in_b, 16)
            sp.dma_start(w2_s[:, :, :, :], w2).then_inc(w2_in, 16)

            def load_groups(lo, hi):
                with sp.Fori(lo, hi) as n:
                    group = x_tok[bass.ds(n, 1)].rearrange("n p h t d -> (n p) h t d")
                    constants_stand(sp)
                    sp.wait_ge(pe_xT, n)
                    sp.dma_start(x_in_v, group).then_inc(xg_in, 16)

            def fill(h):
                sp.wait_ge(fill_ready, h + 1)
                for s in scattered:
                    sp.wait_ge(s, (h + 1) * (16 * HALF_CHOICES // P // 2))
                starts = nc.values_load_multi_w_load_instructions(
                    fill_at[0:1, h, :], (mybir.EngineType.SP,), min_val=0, max_val=HALVES * HALF_ROWS - P,
                    skip_runtime_bounds_check_because="a region has a block's rows to spare")[1]
                for e in range(EXPERTS):
                    sp.dma_start(sorted_rows[bass.ds(starts[e], P), :], fill_rows[:, h * EXPERTS + e, :]
                                 ).then_inc(filled[h], 16)

            load_groups(3, 5)
            sp.wait_ge(fill_rows_ready, 1)
            for h in range(HALVES):
                lo = h * HALF_ROWS + EXPERTS * REGION
                dst = sorted_rows[lo:lo + UNROLL * P, :].rearrange("(u p) r -> p u r", p=P)
                sp.dma_start(dst, fill_rows[:, HALVES * EXPERTS + h * UNROLL:HALVES * EXPERTS + (h + 1) * UNROLL, :]
                             ).then_inc(dummy_out, 16)
            load_groups(5, GROUPS)
            fill(0)

            pair = expert_out[0:CHOICES, :].rearrange("(n h p t) d -> n p h (t d)", n=GROUPS, h=2, p=P)

            def load_pair(b, g, again):
                if again is not None:
                    read = known(sp, again)
                    constants_stand(sp)
                    sp.wait_ge(f_add, read)
                src = pair[g] if isinstance(g, int) else \
                    pair[bass.ds(g, 1)].rearrange("n p h e -> (n p) h e")
                sp.dma_start(pair_in(b), src).then_inc(pair_loaded[b], 16)

            def load_turn(i, m=None):
                rows = nc.values_load_multi_w_load_instructions(
                    blk_row[0:1, bass.ds(i * UNROLL, UNROLL)], (mybir.EngineType.SP,),
                    min_val=0, max_val=HALVES * HALF_ROWS - P,
                    skip_runtime_bounds_check_because="a block lies in its expert's region or among the stand-ins")[1]
                for u in range(UNROLL):
                    if m is not None and u == UNROLL - 3:
                        for b in range(2):
                            load_pair(b, 2 * m + b, None if isinstance(m, int) and m == 0 else 2 * m + b - 1)
                    if not (isinstance(i, int) and i == 0):
                        weighted = known(sp, (i - 1) * UNROLL + u + 1)
                        constants_stand(sp)
                        sp.wait_ge(d_yw, weighted)
                    sp.dma_start(blk_in[:, u, :], sorted_rows[bass.ds(rows[u], P), :]).then_inc(blk_loaded[u], 16)

            sp.wait_ge(dummy_out, 16 * HALVES)
            sp.wait_ge(table_ready, 1)
            sp.wait_ge(filled[0], 16 * EXPERTS)
            load_turn(0)
            with sp.Fori(1, 3) as i:
                load_turn(i)
            fill(1)
            with sp.Fori(3, TURNS // 2) as i:
                load_turn(i)
            sp.wait_ge(table_ready, 2)
            sp.wait_ge(filled[1], 16 * EXPERTS)
            load_turn(TURNS // 2)

            for u in range(UNROLL):
                sp.wait_ge(blk_stored[u], 16 * (TURNS // 2))
            load_turn(FIRST_PAIRS, 0)
            with sp.Fori(1, HALF_PAIRS) as m:
                load_turn(FIRST_PAIRS + m, m)
            load_turn(TURNS - 1)
            for u in range(UNROLL):
                sp.wait_ge(blk_stored[u], 16 * TURNS)
            sp.wait_ge(f_add, HALF_GROUPS)
            with sp.Fori(QUADS, 2 * QUADS) as q:
                for b in range(4):
                    load_pair(b, 4 * q + b, 4 * q + b - 3)
            sp.wait_ge(out_stored, 16 * GROUPS)

        @block.gpsimd
        def _(pool):
            nc.gpsimd.memset(ident[:, :], 0.0).then_inc(c_pool, 1)
            nc.gpsimd.memset(before[:, :], 1.0).then_inc(c_pool, 1)
            nc.gpsimd.memset(head_mask[:, :, :], 1.0).then_inc(c_pool, 1)
            nc.gpsimd.memset(ones_b[:, :], 1.0)
            nc.gpsimd.memset(minus_half[:, :], -0.5)
            nc.gpsimd.memset(ones8[:, :], 1.0)
            nc.gpsimd.memset(bo_split[:, :, :], 0.0)
            pool.wait_ge(c_pool, 3)
            nc.gpsimd.affine_select(out=ident[:, :], in_=ident[:, :], compare_op=ALU.not_equal, fill=1.0,
                                    base=0, pattern=[[-1, P]], channel_multiplier=1).then_inc(c_pool, 1)
            nc.gpsimd.affine_select(out=before[:, :], in_=before[:, :], compare_op=ALU.is_gt, fill=0.0,
                                    base=0, pattern=[[1, P]], channel_multiplier=-1).then_inc(c_pool, 1)
            nc.gpsimd.affine_select(out=head_mask[:, :, :], in_=head_mask[:, :, :], compare_op=ALU.is_ge, fill=0.0,
                                    base=0, pattern=[[-HEAD_DIM, HEADS], [0, HEAD_DIM]],
                                    channel_multiplier=1).then_inc(c_pool, 1)
            pool.wait_ge(c_pool, 6)
            nc.gpsimd.affine_select(out=head_mask[:, :, :], in_=head_mask[:, :, :], compare_op=ALU.is_ge, fill=0.0,
                                    base=HEAD_DIM - 1, pattern=[[HEAD_DIM, HEADS], [0, HEAD_DIM]],
                                    channel_multiplier=-1).then_inc(c_pool, 1)
            nc.gpsimd.iota(iota_ei[:, :], [[1, EXPERTS]], 0, 0)
            nc.gpsimd.iota(tok2_i[:, :], [[2 * SEQ, BATCHES], [TOP_K, 2]], 0, 2 * TOP_K)
            nc.gpsimd.iota(fill_i[:, :], [[P, FILLS]], CHOICES, 1)
            for h in range(HALVES):
                nc.gpsimd.iota(region_i[:, h, :], [[REGION, EXPERTS]], h * HALF_ROWS, 0)
                nc.gpsimd.iota(blk_row_i[:, h, :], [[P, BLOCKS]], h * HALF_ROWS, 0)
            nc.gpsimd.iota(blk_i[:, :], [[1, BLOCKS]], 0, 0).then_inc(c_pool, 1)
            nc.gpsimd.memset(fill_rows[:, :, :], 0.0).then_inc(c_pool, 1)
            pool.wait_ge(c_pool, 9)
            nc.gpsimd.tensor_copy(fill_rows[:, :, DIM:DIM + 1], fill_i[:, :].unsqueeze(2)).then_inc(fill_rows_ready, 1)

            def turn(i, h, par):
                c, d = i - 2, i - 3

                def scatter(t, k):
                    pool.indirect_dma_start(
                        out=sorted_rows[:, :],
                        out_offset=bass.IndirectOffsetOnAxis(
                            ap=slots[:, 1 - par, t, k:k + 1], axis=0),
                        in_=rows_now[:, 1 - par, t, :],
                        in_offset=None).then_inc(scattered[1 - par], 16)

                if live(c):
                    pool.wait_ge(dv_eps, c + 1)
                    nc.gpsimd.tensor_tensor(rstd[:, :], var_eps[:, :], minus_half[:, :], ALU.pow).then_inc(pl_rstd, 1)
                if live(d):
                    ready = known(pool, d + 1)
                    constants_stand(pool)
                    pool.wait_ge(dv_slot, ready)
                    pool.wait_ge(dv_pay, ready)
                    for t in range(GT):
                        scatter(t, 0)
                        scatter(t, 1)
            pool.wait_ge(c_dve, CONSTANTS)
            stage_a_turns(pool, turn)

            def inverse_std(b, g, again):
                if again is not None:
                    pool.wait_ge(f_fin, again)
                pool.wait_ge(f_eps, g + 1)
                nc.gpsimd.tensor_tensor(rstd2[:, b, :], var_eps2[:, b, :], minus_half[:, :],
                                        ALU.pow).then_inc(f_rstd, 1)

            def store_turn(i, m=None):
                for u in range(UNROLL):
                    if m is not None and u in (4, 10):
                        b = u // 10
                        inverse_std(b, 2 * m + b, None if isinstance(m, int) and m == 0 else 2 * m + b - 1)
                    read = known(pool, i * 2 + (1 if u < UNROLL // 2 else 2))
                    weighted = known(pool, i * UNROLL + u + 1)
                    constants_stand(pool)
                    pool.wait_ge(d_pay, read)
                    pool.wait_ge(d_yw, weighted)
                    pool.indirect_dma_start(
                        out=expert_out[:, :],
                        out_offset=bass.IndirectOffsetOnAxis(ap=blk_dst[:, u:u + 1], axis=0),
                        in_=blk_out[:, u, :], in_offset=None).then_inc(blk_stored[u], 16)

            with pool.Fori(0, FIRST_PAIRS) as i:
                store_turn(i)
            store_turn(FIRST_PAIRS, 0)
            with pool.Fori(1, HALF_PAIRS) as m:
                store_turn(m + FIRST_PAIRS, m)
            store_turn(TURNS - 1)
            pool.wait_ge(f_fin, HALF_GROUPS)
            with pool.Fori(QUADS, 2 * QUADS) as q:
                for b in range(4):
                    inverse_std(b, 4 * q + b, 4 * q + b - 3)

        @block.scalar
        def _(act):
            act.wait_ge(rest_in, 16)
            nc.scalar.activation(proj_hi[:, Q:K + 1, :], rest_s[:, 0:2 * DIM].rearrange("p (n d) -> p n d", n=2),
                                 ACT.Copy).then_inc(c_act, 1)
            nc.scalar.activation(router_s[:, :], router_in, ACT.Copy, scale=2.0).then_inc(c_act, 1)
            act.wait_ge(c_pe, 2)
            nc.scalar.activation(proj_hi[:, QR, :], B[0][:, 0:P], ACT.Copy).then_inc(c_act, 1)
            nc.scalar.activation(proj_hi[:, KR, :], B[1][:, 0:P], ACT.Copy).then_inc(c_act, 1)
            nc.scalar.activation(bqr[:, :], B[0][:, P:P + 1], ACT.Copy).then_inc(c_act, 1)
            nc.scalar.activation(bkr[:, :], B[1][:, P:P + 1], ACT.Copy).then_inc(c_act, 1)
            act.wait_ge(c_act, 6)

            def round_weights(experts):
                for e in experts:
                    nc.scalar.activation(w13_hi[:, e, :], w13_s[:, e, :], ACT.Copy, scale=2.0).then_inc(w13_h, 1)

            def turn(i, h, par):
                n, a, b, c = i + 1, i, i - 1, i - 2
                if live(a):
                    act.wait_ge(pe_q, a + 1)
                    nc.scalar.activation(q_sq[:, :], B[1][:, :], ACT.Square, bias=bq_s[:, :]).then_inc(ac_sq, 1)
                if live(b):
                    act.wait_ge(pe_kT, b + 1)
                    nc.scalar.activation(k_tok[:, :, :], B[3][:, :].rearrange("p (t d) -> p t d", t=GT),
                                         ACT.Copy).then_inc(ac_kT, 1)
                if live(a):
                    act.wait_ge(ac_sq, 2 * a + 1)
                    nc.scalar.activation(q_sq_hi[:, :], q_sq[:, :], ACT.Copy).then_inc(ac_q2, 1)
                    act.wait_ge(pe_k, a + 1)
                    nc.scalar.activation(k_sq[:, :], B[2][:, :], ACT.Square, bias=bk_s[:, :]).then_inc(ac_sq, 1)
                    act.wait_ge(ac_sq, 2 * a + 2)
                    nc.scalar.activation(k_sq_hi[:, :], k_sq[:, :], ACT.Copy).then_inc(ac_k2, 1)
                if live(c):
                    act.wait_ge(dv_shift, c + 1)
                    if not (isinstance(c, int) and c < 2):
                        act.wait_ge(scattered[par], (c - par) * (8 * TOP_K * GT))
                    for t in range(GT):
                        st = nc.scalar.activation(rows_now[:, par, t, 0:DIM], resid[:, t, :], ACT.Identity,
                                                  bias=shift[:, t:t + 1], scale=rstd[:, t:t + 1])
                    st.then_inc(ac_rows, 1)
                if live(a):
                    act.wait_ge(pe_fq, a + 1)
                    if not first(a):
                        act.wait_ge(pe_att, a)
                    nc.scalar.activation(q_feat[:, :], B[1][:, :], ACT.Exp, bias=bqr[:, :]).then_inc(ac_fq, 1)
                if live(n):
                    act.wait_ge(pe_xT, n + 1)
                    nc.scalar.activation(xT_hi[:, 1 - par, :], B[0][:, :], ACT.Copy)
                    nc.scalar.activation(xT[:, 1 - par, :], B[0][:, :], ACT.Copy).then_inc(ac_xT, 1)
                if live(c):
                    act.wait_ge(pe_x2T, c + 1)
                    nc.scalar.activation(x2T[:, :, :], B[6][:, :].rearrange("p (t d) -> p t d", t=GT),
                                         ACT.Copy).then_inc(ac_x2T, 1)
                if live(a):
                    act.wait_ge(pe_fk, a + 1)
                    nc.scalar.activation(k_feat[:, :], B[2][:, :], ACT.Exp, bias=bkr[:, :]).then_inc(ac_fk, 1)
                if live(b):
                    act.wait_ge(pe_attT, b + 1)
                    nc.scalar.activation(attnT[:, :, :], B[4][:, :].rearrange("p (t d) -> p t d", t=GT),
                                         ACT.Copy).then_inc(ac_attT, 1)
                if live(c):
                    act.wait_ge(dv_gap, c + 1)
                    nc.scalar.activation(exp8[:, :, :], gap8[:, :, :], ACT.Exp).then_inc(ac_exp8, 1)
                if isinstance(i, int) and 0 <= i < 4:
                    act.wait_ge(w13_in, 16)
                    round_weights(range(i * EXPERTS // 4, (i + 1) * EXPERTS // 4))

            stage_a_turns(act, turn)

            def silu(j, u):
                act.wait_ge(d_h, j + 1)
                nc.scalar.activation(silu_g[:, u % 2, :], B[u % 2][:, 0:INNER], ACT.Silu).then_inc(d_silu, 1)

            def hidden_out(j, u):
                act.wait_ge(d_hT, j + 1)
                nc.scalar.activation(hiddenT[:, u % 2, :], B[2 + u % 2][:, 0:INNER], ACT.Copy).then_inc(d_hTc, 1)

            def round_x(j, u):
                act.wait_ge(d_xT, j + 1)
                nc.scalar.activation(blk_xT_hi[:, u % 2, :], B[4 + u % 2][:, 0:P], ACT.Copy).then_inc(d_xTh, 1)

            out_v = out.rearrange("(n h) (p t) d -> n p h t d", n=GROUPS, h=2, t=2)

            def finish_tile(b, g, t):
                if t == 0:
                    shifted = known(act, g + 1)
                    constants_stand(act)
                    act.wait_ge(f_shift, shifted)
                mine = x_all[:, bass.ds(g * GT, GT), :]
                st = nc.scalar.activation(mine[:, t, :], mine[:, t, :], ACT.Identity,
                                          bias=shift2[:, b, t:t + 1], scale=rstd2[:, b, t:t + 1])
                if t == GT - 1:
                    st.then_inc(f_fin, 1)
                    act.wait_ge(f_fin, g + 1)
                    dst = out_v[g] if isinstance(g, int) else out_v[bass.ds(g, 1)].rearrange("n p h t d -> (n p) h t d")
                    act.dma_start(dst, mine.rearrange("p (h t) d -> p h t d", h=2)).then_inc(out_stored, 16)

            def expert_turn(i, start, end, m=None, late=None):
                if start:
                    round_x(0, 0)
                    round_x(1, 1)
                for u in range(UNROLL):
                    j = i * UNROLL + u
                    silu(j, u)
                    if not (end and u >= UNROLL - 2):
                        round_x(j + 2, u)
                    if not (start and u == 0):
                        hidden_out(j - 1, (u - 1) % 2)
                    if m is not None and u >= 8:
                        finish_tile(0, 2 * m, u - 8)
                    if late is not None and 3 <= u < 7:
                        finish_tile(1, late, u - 3)

            expert_turn(0, True, False)
            with act.Fori(1, FIRST_PAIRS) as i:
                expert_turn(i, False, False)
            expert_turn(FIRST_PAIRS, False, False, 0)
            with act.Fori(1, HALF_PAIRS) as m:
                expert_turn(m + FIRST_PAIRS, False, False, m, 2 * m - 1)
            expert_turn(TURNS - 1, False, True, None, HALF_GROUPS - 1)
            hidden_out(TURNS * UNROLL - 1, 1)
            with act.Fori(QUADS, 2 * QUADS) as q:
                for b in range(4):
                    for t in range(GT):
                        finish_tile(b, 4 * q + b, t)

        @block.vector
        def _(dve):
            dve.wait_ge(c_pool, 8)
            hm = head_mask[:, :, :].rearrange("p h d -> p (h d)")
            nc.vector.tensor_scalar(neg_half_sum[:, :], hm, -0.5 / HEAD_DIM, None, ALU.mult).then_inc(c_dve, 1)
            nc.vector.tensor_copy(iota_e[:, :], iota_ei[:, :]).then_inc(c_dve, 1)
            nc.vector.tensor_copy(tok2_f[:, :], tok2_i[:, :]).then_inc(c_dve, 1)
            nc.vector.tensor_copy(region_f[:, :, :], region_i[:, :, :]).then_inc(c_dve, 1)
            nc.vector.tensor_copy(blk_f[:, :], blk_i[:, :]).then_inc(c_dve, 1)
            nc.vector.tensor_copy(blk_row_f[:, :, :], blk_row_i[:, :, :]).then_inc(c_dve, 1)
            nc.vector.tensor_copy(place[:, 0, GT, :], region_i[:, 0, :]).then_inc(c_dve, 1)
            nc.vector.tensor_copy(place[:, HALF_GROUPS + 1, GT, :], region_i[:, 1, :]).then_inc(c_dve, 1)
            nc.vector.tensor_copy(kv_den[:, 0, DIM:DIM + HEADS], head_mask[:, :, 0]).then_inc(c_dve, 1)
            nc.vector.tensor_copy(kv_den[:, 1, DIM:DIM + HEADS], head_mask[:, :, 0]).then_inc(c_dve, 1)
            dve.wait_ge(fold_in, 16)
            nc.vector.scalar_tensor_tensor(blk_r[:, :], r_s[:, :], float(HEAD_DIM) ** -0.5, hm,
                                           ALU.mult, ALU.mult).then_inc(c_dve, 1)
            dve.wait_ge(rest_in, 16)
            nc.vector.tensor_copy(bo_split[0:1, :, :], bc(bo_s[0:1, :], 1, [1, GT, DIM])).then_inc(c_dve, 1)
            dve.wait_ge(c_dve, 12)
            nc.vector.tensor_tensor(bo_rest[0:1, 0, :], bo_s[0:1, :], bo_split[0:1, 0, :],
                                    ALU.subtract).then_inc(c_dve, 1)
            dve.wait_ge(c_dve, 13)
            nc.vector.tensor_copy(bo_split[32:33, :, :], bc(bo_rest[0:1, 0, :], 1, [1, GT, DIM])).then_inc(c_dve, 1)
            dve.wait_ge(c_dve, 14)
            nc.vector.tensor_copy(bo_rest[32:33, 0, :], bo_rest[0:1, 0, :]).then_inc(c_dve, 1)
            dve.wait_ge(c_dve, 15)
            nc.vector.tensor_tensor(bo_rest[32:33, 1, :], bo_rest[32:33, 0, :], bo_split[32:33, 0, :],
                                    ALU.subtract).then_inc(c_dve, 1)
            dve.wait_ge(c_dve, 16)
            nc.vector.tensor_copy(bo_split[64:65, :, :], bc(bo_rest[32:33, 1, :], 1, [1, GT, DIM])).then_inc(c_dve, 1)

            dve.wait_ge(c_act, 1)
            nc.vector.tensor_tensor(proj_lo[:, Q:K + 1, :], rest_s[:, 0:2 * DIM].rearrange("p (n d) -> p n d", n=2),
                                    proj_hi[:, Q:K + 1, :].bitcast(F32), ALU.subtract).then_inc(c_dve, 1)
            dve.wait_ge(c_act, 6)
            nc.vector.tensor_tensor(proj_lo[:, QR, :], B[0][:, 0:P], proj_hi[:, QR, :].bitcast(F32),
                                    ALU.subtract).then_inc(c_dve, 1)
            nc.vector.tensor_tensor(proj_lo[:, KR, :], B[1][:, 0:P], proj_hi[:, KR, :].bitcast(F32),
                                    ALU.subtract).then_inc(c_dve, 1)

            def turn(i, h, par):
                n, a, b, c, d = i + 1, i, i - 1, i - 2, i - 3
                if live(c):
                    dve.wait_ge(pe_wo, c + 1)
                    if isinstance(c, int) and c < 3:
                        dve.wait_ge(x_in_a, 16 * 3)
                    else:
                        dve.wait_ge(x_in_b, 16 * (GROUPS - 3))
                    nc.vector.tensor_tensor(resid[:, :, :], B[5][:, :].rearrange("p (t d) -> p t d", t=GT),
                                            x_all[:, bass.ds(c * GT, GT), :], ALU.add).then_inc(dv_res, 1)
                    dve.wait_ge(dv_res, c + 1)
                    for t in range(GT):
                        st = nc.vector.bn_stats(stats[:, t, :], resid[:, t, :])
                    st.then_inc(dv_stat, 1)
                    constants_stand(dve)
                    dve.wait_ge(dv_stat, c + 1)
                    for t in range(GT):
                        st = nc.vector.bn_aggr(meanvar[:, t, :], stats[:, t, :])
                    st.then_inc(dv_mv, 1)
                    dve.wait_ge(dv_mv, c + 1)
                    nc.vector.tensor_scalar(var_eps[:, :], meanvar[:, :, 1], 4.0, 4.0 * LN_EPS,
                                            ALU.mult, ALU.add).then_inc(dv_eps, 1)
                if live(a):
                    dve.wait_ge(ac_q2, a + 1)
                    nc.vector.tensor_tensor(q_sq_lo[:, :], q_sq[:, :], q_sq_hi[:, :].bitcast(F32),
                                            ALU.subtract).then_inc(dv_q2, 1)
                if live(d):
                    dve.wait_ge(pe_place, d + 1)
                    nc.vector.tensor_tensor(
                        place[:, bass.ds(d + h + 1, 1), :, :].rearrange("p a t e -> p (a t) e"),
                        B[7][:, 64:64 + (GT + 1) * EXPERTS].rearrange("p (t e) -> p t e", e=EXPERTS),
                        place[:, bass.ds(d + h, 1), GT, :].to_broadcast([P, GT + 1, EXPERTS]),
                        ALU.add).then_inc(dv_place, 1)
                    dve.wait_ge(ac_exp8, d + 1)
                    nc.vector.tensor_reduce(sum8[:, :], exp8[:, :, :], AX_X, ALU.add).then_inc(dv_sum, 1)
                    dve.wait_ge(dv_place, d + 1)
                    nc.vector.tensor_tensor(
                        picked[:, :, :, :], chosen[:, :, :, :],
                        place[:, bass.ds(d + h + 1, 1), 0:GT, :].to_broadcast([P, TOP_K, GT, EXPERTS]),
                        ALU.mult).then_inc(dv_pick, 1)
                    dve.wait_ge(dv_sum, d + 1)
                    nc.vector.tensor_scalar(wden[:, :], sum8[:, :], 1e-6, 1.0, ALU.mult, ALU.add).then_inc(dv_wd, 1)
                    dve.wait_ge(dv_pick, d + 1)
                    with nc.allow_low_precision(reason="row numbers are whole and below 2**24"):
                        nc.vector.tensor_reduce(
                            slots[:, 1 - par, :, :].rearrange("p t k -> p k t"),
                            picked[:, :, :, :], AX_X, ALU.add).then_inc(dv_slot, 1)
                    dve.wait_ge(dv_wd, d + 1)
                    nc.vector.tensor_tensor(wden2[:, :], wden[:, :], exp8[:, :, 1], ALU.add).then_inc(dv_wd2, 1)
                    pay = rows_now[:, 1 - par, :, :]
                    nc.vector.tensor_copy(pay[:, :, DIM:DIM + 1], tok2_f[:, bass.ds(d * GT, GT)].unsqueeze(2))
                    nc.vector.tensor_copy(pay[:, :, DIM + 1:DIM + 2], idx8[:, :, 1:2])
                    dve.wait_ge(dv_wd2, d + 1)
                    nc.vector.reciprocal(pay[:, :, DIM + 2:DIM + 3], wden2[:, :].unsqueeze(2)).then_inc(dv_w1, 1)
                if live(c):
                    dve.wait_ge(pl_rstd, c + 1)
                    nc.vector.scalar_tensor_tensor(shift[:, :], meanvar[:, :, 0], -1.0, rstd[:, :],
                                                   ALU.mult, ALU.mult).then_inc(dv_shift, 1)
                if live(b):
                    dve.wait_ge(pe_kv, b + 1)
                    nc.vector.tensor_tensor(
                        kv_den[:, :, 0:DIM], B[3][:, 0:2 * DIM].rearrange("p (a d) -> p a d", a=2),
                        bc(hm, 1, [P, 2, DIM]), ALU.mult).then_inc(dv_kv, 1)
                if live(d):
                    dve.wait_ge(dv_w1, d + 1)
                    nc.vector.scalar_tensor_tensor(pay[:, :, DIM + 3:DIM + 4], exp8[:, :, 1:2], -1.0,
                                                   pay[:, :, DIM + 2:DIM + 3], ALU.add, ALU.mult).then_inc(dv_pay, 1)
                if isinstance(i, int) and i == GROUPS:
                    table_counts(0)
                if live(a):
                    dve.wait_ge(ac_k2, a + 1)
                    nc.vector.tensor_tensor(k_sq_lo[:, :], k_sq[:, :], k_sq_hi[:, :].bitcast(F32),
                                            ALU.subtract).then_inc(dv_k2, 1)
                    dve.wait_ge(pe_v, a + 1)
                    nc.vector.tensor_tensor(v_tok[:, :, :], B[0][:, :].rearrange("p (t d) -> p t d", t=GT),
                                            bc(bv_s[:, :], 1, [P, GT, DIM]), ALU.add).then_inc(dv_v, 1)
                if live(b):
                    dve.wait_ge(pe_att, b + 1)
                    att = [B[4 + m][:, 0:2 * (DIM + HEADS)].rearrange("p (t d) -> p t d", t=2) for m in range(2)]
                    for m in range(2):
                        st = nc.vector.tensor_scalar(den[:, 2 * m:2 * m + 2, :], att[m][:, :, DIM:DIM + HEADS],
                                                     1e-8, None, ALU.add)
                    st.then_inc(dv_den, 1)
                    dve.wait_ge(dv_den, b + 1)
                    nc.vector.reciprocal(zrec[:, :, :], den[:, :, :]).then_inc(dv_z, 1)
                    dve.wait_ge(dv_z, b + 1)
                    for m in range(2):
                        st = nc.vector.tensor_tensor(
                            attn[:, 2 * m:2 * m + 2, :].rearrange("p t (h e) -> p t h e", h=HEADS),
                            att[m][:, :, 0:DIM].rearrange("p t (h e) -> p t h e", h=HEADS),
                            bc(zrec[:, 2 * m:2 * m + 2, :], 3, [P, 2, HEADS, HEAD_DIM]), ALU.mult)
                    st.then_inc(dv_att, 1)
                if live(n):
                    dve.wait_ge(ac_xT, n + 1)
                    nc.vector.tensor_tensor(xT_lo[:, 1 - par, :], xT[:, 1 - par, :], xT_hi[:, 1 - par, :].bitcast(F32),
                                            ALU.subtract).then_inc(dv_xT, 1)
                if isinstance(i, int) and i == GROUPS:
                    table_blocks(0)
                if live(c):
                    constants_stand(dve)
                    dve.wait_ge(pe_logit, c + 1)
                    for t in range(GT):
                        st = nc.vector.max(top8[:, t, :], B[7][:, t * EXPERTS:(t + 1) * EXPERTS])
                    st.then_inc(dv_top, 1)
                    constants_stand(dve)
                    dve.wait_ge(dv_top, c + 1)
                    for t in range(GT):
                        st = nc.vector.max_index(idx8[:, t, :], top8[:, t, :], B[7][:, t * EXPERTS:(t + 1) * EXPERTS])
                    st.then_inc(dv_idx, 1)
                    nc.vector.tensor_tensor(gap8[:, :, :], top8[:, :, :], top8[:, :, 0:1].to_broadcast([P, GT, 8]),
                                            ALU.subtract).then_inc(dv_gap, 1)
                    dve.wait_ge(dv_idx, c + 1)
                    nc.vector.tensor_tensor(
                        chosen[:, :, :, :],
                        bc(idx8[:, :, 0:TOP_K].rearrange("p t k -> p k t"), 3, [P, TOP_K, GT, EXPERTS]),
                        iota_e[:, :].unsqueeze(1).unsqueeze(1).to_broadcast([P, TOP_K, GT, EXPERTS]),
                        ALU.is_equal).then_inc(dv_cho, 1)
                    dve.wait_ge(dv_cho, c + 1)
                    nc.vector.tensor_tensor(either[:, :, :], chosen[:, 0, :, :], chosen[:, 1, :, :],
                                            ALU.add).then_inc(dv_both, 1)
                if isinstance(i, int) and 0 <= i < 4:
                    for e in range(i * EXPERTS // 4, (i + 1) * EXPERTS // 4):
                        dve.wait_ge(w13_h, e + 1)
                        nc.vector.scalar_tensor_tensor(w13_lo[:, e, :], w13_s[:, e, :], 2.0,
                                                       w13_hi[:, e, :].bitcast(F32),
                                                       ALU.mult, ALU.subtract).then_inc(w13_l, 1)

            def table_counts(h):
                n = 9 * h
                ends = place[:, (h + 1) * (HALF_GROUPS + 1) - 1, GT, :]
                nc.vector.tensor_copy(fill_at[:, h, :], ends).then_inc(fill_ready, 1)
                nc.vector.tensor_tensor(count_f[:, :], ends, region_f[:, h, :], ALU.subtract).then_inc(tb, 1)
                dve.wait_ge(tb, n + 1)
                nc.vector.tensor_scalar(count_i[:, :], count_f[:, :], float(P - 1), None, ALU.add).then_inc(tb, 1)
                dve.wait_ge(tb, n + 2)
                nc.vector.tensor_scalar(nblk_i[:, :], count_i[:, :], P.bit_length() - 1, None,
                                        ALU.arith_shift_right).then_inc(tb, 1)
                dve.wait_ge(tb, n + 3)
                nc.vector.tensor_copy(nblk_f[:, :], nblk_i[:, :]).then_inc(tb, 1)
                dve.wait_ge(tb, n + 4)
                nc.vector.tensor_tensor_scan(end_f[:, :], ones8[:, :], nblk_f[:, :], 0.0,
                                             ALU.mult, ALU.add).then_inc(tb, 1)
                nc.vector.tensor_scalar(skip_f[:, :], nblk_f[:, :], -float(P), float(REGION),
                                        ALU.mult, ALU.add).then_inc(tb, 1)

            def table_blocks(h):
                n = 9 * h
                dve.wait_ge(tb, n + 6)
                shape = [P, BLOCKS, EXPERTS]
                nc.vector.tensor_tensor(past[:, :, :], bc(end_f[:, :], 1, shape), bc(blk_f[:, :], 2, shape),
                                        ALU.is_le).then_inc(tb, 1)
                dve.wait_ge(tb, n + 7)
                nc.vector.tensor_tensor(past_skip[:, :, :], past[:, :, :], bc(skip_f[:, :], 1, shape),
                                        ALU.mult).then_inc(tb, 1)
                mine = slice(h * BLOCKS, (h + 1) * BLOCKS)
                nc.vector.tensor_reduce(blk_expert[:, mine], past[:, :, :], AX_X, ALU.add)
                dve.wait_ge(tb, n + 8)
                nc.vector.tensor_reduce(blk_skip[:, :], past_skip[:, :, :], AX_X, ALU.add).then_inc(tb, 1)
                dve.wait_ge(tb, n + 9)
                nc.vector.tensor_scalar(blk_expert_i[:, LEAD + h * BLOCKS:LEAD + (h + 1) * BLOCKS], blk_expert[:, mine], float(EXPERTS - 1), None, ALU.min)
                nc.vector.tensor_tensor(blk_row[:, mine], blk_skip[:, :], blk_row_f[:, h, :],
                                        ALU.add).then_inc(table_ready, 1)

            stage_a_turns(dve, turn)

            def xT_copy(j, u):
                dve.wait_ge(d_xTh, j + 1)
                nc.vector.tensor_tensor(blk_xT_lo[:, u % 2, :], B[4 + u % 2][:, 0:P],
                                        blk_xT_hi[:, u % 2, :].bitcast(F32), ALU.subtract).then_inc(d_xTc, 1)

            def gate_up(j, u):
                dve.wait_ge(d_silu, j + 1)
                nc.vector.tensor_tensor(hidden[:, u % 2, :], silu_g[:, u % 2, :], B[u % 2][:, INNER:2 * INNER],
                                        ALU.mult).then_inc(d_mul, 1)

            def weigh(j, u, again):
                dve.wait_ge(d_y, j + 1)
                if again is not None:
                    dve.wait_ge(blk_stored[u], again)
                nc.vector.scalar_tensor_tensor(blk_out[:, u, :], B[6 + u % 2][:, 0:DIM], blk_w[:, u:u + 1],
                                               blk_in[:, u, 0:DIM], ALU.mult, ALU.add).then_inc(d_yw, 1)

            def payload(i, part, start):
                s = slice(part * UNROLL // 2, (part + 1) * UNROLL // 2)
                for u in range(s.start, s.stop):
                    dve.wait_ge(blk_loaded[u], 16 * (i + 1))
                    if not start:
                        dve.wait_ge(blk_stored[u], 16 * i)
                nc.vector.tensor_tensor(is_second[:, s], blk_in[:, s, DIM + 1],
                                        blk_expert[:, bass.ds(i * UNROLL + s.start, UNROLL // 2)],
                                        ALU.is_equal).then_inc(d_chain, 1)
                dve.wait_ge(d_chain, (i * 2 + part) * 2 + 1)
                nc.vector.tensor_tensor(w_diff[:, s], is_second[:, s], blk_in[:, s, DIM + 3],
                                        ALU.mult).then_inc(d_chain, 1)
                nc.vector.tensor_tensor(blk_dst[:, s], is_second[:, s], blk_in[:, s, DIM], ALU.add)
                dve.wait_ge(d_chain, (i * 2 + part) * 2 + 2)
                nc.vector.tensor_tensor(blk_w[:, s], w_diff[:, s], blk_in[:, s, DIM + 2],
                                        ALU.add).then_inc(d_pay, 1)

            def pair_sum(b, g, loads, half):
                if half == 0:
                    dve.wait_ge(pair_loaded[b], 16 * loads)
                pr = pair_in(b)[:, half, :].rearrange("p (t k d) -> p t k d", t=2, k=TOP_K)
                st = nc.vector.tensor_tensor(x_all[:, bass.ds(g * GT + 2 * half, 2), :],
                                             pr[:, :, 0, :], pr[:, :, 1, :], ALU.add)
                if half == 1:
                    st.then_inc(f_add, 1)

            def pair_stats(b, g, half):
                if half == 0:
                    added = known(dve, g + 1)
                    constants_stand(dve)
                    dve.wait_ge(f_add, added)
                mine = x_all[:, bass.ds(g * GT + 2 * half, 2), :]
                for t in range(2):
                    st = nc.vector.bn_stats(stats2[:, b, 2 * half + t, :], mine[:, t, :])
                if half == 1:
                    st.then_inc(f_stat, 1)

            def pair_var(b, g):
                measured = known(dve, g + 1)
                constants_stand(dve)
                dve.wait_ge(f_stat, measured)
                for t in range(GT):
                    st = nc.vector.bn_aggr(meanvar2[:, b, t, :], stats2[:, b, t, :])
                st.then_inc(f_mv, 1)
                dve.wait_ge(f_mv, g + 1)
                nc.vector.tensor_scalar(var_eps2[:, b, :], meanvar2[:, b, :, 1], LN_EPS, None,
                                        ALU.add).then_inc(f_eps, 1)

            def pair_shift(b, g):
                dve.wait_ge(f_rstd, g + 1)
                nc.vector.scalar_tensor_tensor(shift2[:, b, :], meanvar2[:, b, :, 0], -1.0, rstd2[:, b, :],
                                               ALU.mult, ALU.mult).then_inc(f_shift, 1)

            def expert_turn(i, start, end, m=None, late=None):
                if start:
                    xT_copy(0, 0)
                    xT_copy(1, 1)
                for u in range(UNROLL):
                    j = i * UNROLL + u
                    gate_up(j, u)
                    if not (end and u >= UNROLL - 2):
                        xT_copy(j + 2, u)
                    if not (start and u < 2):
                        su = (u - 2) % UNROLL
                        again = None if (start or (u < 2 and isinstance(i, int) and i == 1)) else \
                            (16 * i if u >= 2 else 16 * (i - 1))
                        if su == 0:
                            dve.wait_ge(d_pay, 2 * i + 1)
                        elif su == UNROLL // 2:
                            dve.wait_ge(d_pay, 2 * i + 2)
                        weigh(j - 2, su, again)
                    if u == 1:
                        payload(i, 0, start)
                    if u == 1 + UNROLL // 2:
                        payload(i, 1, start)
                    if u == 3 and isinstance(i, int) and i == 1:
                        table_counts(1)
                    if u == 5 and isinstance(i, int) and i == 1:
                        table_blocks(1)
                    if m is not None:
                        g = 2 * m
                        if u in (0, 2):
                            pair_sum(0, g, m + 1, u // 2)
                        if u in (3, 4):
                            pair_stats(0, g, u - 3)
                        if u == 5:
                            pair_var(0, g)
                        if u in (6, 8):
                            pair_sum(1, g + 1, m + 1, u // 2 - 3)
                        if u in (9, 10):
                            pair_stats(1, g + 1, u - 9)
                        if u == 11:
                            pair_var(1, g + 1)
                        if u == 7:
                            pair_shift(0, g)
                    if late is not None and u == 2:
                        pair_shift(1, late)

            expert_turn(0, True, False)
            expert_turn(1, False, False)
            with dve.Fori(2, FIRST_PAIRS) as i:
                expert_turn(i, False, False)
            expert_turn(FIRST_PAIRS, False, False, 0)
            with dve.Fori(1, HALF_PAIRS) as m:
                expert_turn(m + FIRST_PAIRS, False, False, m, 2 * m - 1)
            expert_turn(TURNS - 1, False, True, None, HALF_GROUPS - 1)
            weigh(TURNS * UNROLL - 2, UNROLL - 2, 16 * (TURNS - 1))
            weigh(TURNS * UNROLL - 1, UNROLL - 1, 16 * (TURNS - 1))

            def quad_turn(q, start):
                for b in range(4):
                    g = 4 * q + b
                    for half in range(2):
                        pair_sum(b, g, HALF_PAIRS + q - QUADS + 1 if b < 2 else q - QUADS + 1, half)
                    for half in range(2):
                        pair_stats(b, g, half)
                    if not (start and b == 0):
                        pair_shift((b - 1) % 4, g - 1)
                    pair_var(b, g)

            quad_turn(QUADS, True)
            with dve.Fori(QUADS + 1, 2 * QUADS) as q:
                quad_turn(q, False)
            pair_shift(3, GROUPS - 1)

        @block.tensor
        def _(pe):
            pe.wait_ge(c_dve, 11)
            nc.tensor.matmul(B[0][:, 0:P], wq_s[:, :], blk_r[:, :], start=True, stop=True)
            nc.tensor.matmul(B[0][:, P:P + 1], blk_r[:, :], bq_s[:, :], start=True, stop=True).then_inc(c_pe, 1)
            nc.tensor.matmul(B[1][:, 0:P], wk_s[:, :], blk_r[:, :], start=True, stop=True)
            nc.tensor.matmul(B[1][:, P:P + 1], blk_r[:, :], bk_s[:, :], start=True, stop=True).then_inc(c_pe, 1)
            pe.wait_ge(c_act, 6)
            pe.wait_ge(c_dve, 20)

            def project(bank, par, which, stop=True):
                parts = [(proj_hi, xT_hi), (proj_lo, xT_hi), (proj_hi, xT_lo)]
                for p, (weights, moving) in enumerate(parts):
                    mm = nc.tensor.matmul(B[bank][:, :], weights[:, which, :], moving[:, par, :],
                                          start=(p == 0), stop=(stop and p == 2))
                return mm

            def turn(i, h, par):
                n, a, b, c, d = i + 1, i, i - 1, i - 2, i - 3
                if live(a):
                    pe.wait_ge(dv_xT, a + 1)
                    if not first(a):
                        pe.wait_ge(ac_fq, a)
                    project(1, par, Q).then_inc(pe_q, 1)
                if live(b):
                    pe.wait_ge(ac_fk, b + 1)
                    if not first(b):
                        pe.wait_ge(dv_kv, b)
                    for t in range(GT):
                        mm = nc.tensor.transpose(B[3][:, t * P:(t + 1) * P], k_feat[:, t * P:(t + 1) * P], ident[:, :])
                    mm.then_inc(pe_kT, 1)
                if live(a):
                    if not first(a):
                        pe.wait_ge(ac_fk, a)
                    project(2, par, K).then_inc(pe_k, 1)
                if live(d):
                    pe.wait_ge(dv_both, d + 1)
                    at = 64
                    nc.tensor.matmul(B[7][:, at:at + GT * EXPERTS], before[:, :],
                                     either[:, :, :].rearrange("p t e -> p (t e)"), start=True, stop=False,
                                     skip_group_check=True)
                    for t in range(GT):
                        lo = (t + 1) * EXPERTS
                        mm = nc.tensor.matmul(B[7][:, at + lo:at + (GT + 1) * EXPERTS], ones_b[:, :],
                                              either[:, 0:GT - t, :].rearrange("p t e -> p (t e)"),
                                              start=False, stop=(t == GT - 1), skip_group_check=True)
                    mm.then_inc(pe_place, 1)
                if live(b):
                    pe.wait_ge(ac_kT, b + 1)
                    pe.wait_ge(dv_v, b + 1)
                    for m in range(2):
                        for t in range(2):
                            mm = nc.tensor.matmul(B[3][:, m * DIM:(m + 1) * DIM], k_tok[:, 2 * m + t, :],
                                                  v_tok[:, 2 * m + t, :], start=(t == 0), stop=(t == 1))
                    mm.then_inc(pe_kv, 1)
                if live(a):
                    pe.wait_ge(ac_q2, a + 1)
                    project(1, par, QR, stop=False)
                    pe.wait_ge(dv_q2, a + 1)
                    nc.tensor.matmul(B[1][:, :], neg_half_sum[:, :], q_sq_hi[:, :], start=False, stop=False)
                    nc.tensor.matmul(B[1][:, :], neg_half_sum[:, :], q_sq_lo[:, :], start=False, stop=True).then_inc(pe_fq, 1)
                    for t in range(GT):
                        mm = nc.tensor.matmul(B[0][:, t * P:(t + 1) * P], xT[:, par, t * P:(t + 1) * P], wvT_s[:, :],
                                              start=True, stop=True)
                    mm.then_inc(pe_v, 1)
                if live(b):
                    pe.wait_ge(ac_fq, b + 1)
                    pe.wait_ge(dv_kv, b + 1)
                    if not first(b):
                        pe.wait_ge(ac_attT, b)
                        pe.wait_ge(dv_res, b)
                    for t in range(GT):
                        mm = nc.tensor.matmul(B[4 + t // 2][:, (t % 2) * (DIM + HEADS):(t % 2 + 1) * (DIM + HEADS)],
                                              q_feat[:, t * P:(t + 1) * P], kv_den[:, t // 2, :], start=True, stop=True)
                    mm.then_inc(pe_att, 1)
                if live(n):
                    pe.wait_ge(xg_in, 16 * (n + 1))
                    if live(a):
                        pe.wait_ge(dv_v, a + 1)
                    for t in range(GT):
                        mm = nc.tensor.transpose(B[0][:, t * P:(t + 1) * P], x_in[:, t, :], ident[:, :])
                    mm.then_inc(pe_xT, 1)
                if live(c):
                    pe.wait_ge(ac_rows, c + 1)
                    if not first(c):
                        pe.wait_ge(ac_x2T, c)
                    for t in range(GT):
                        mm = nc.tensor.transpose(B[6][:, t * P:(t + 1) * P], rows_now[:, par, t, 0:DIM], ident[:, :])
                    mm.then_inc(pe_x2T, 1)
                if live(a):
                    pe.wait_ge(ac_k2, a + 1)
                    project(2, par, KR, stop=False)
                    pe.wait_ge(dv_k2, a + 1)
                    nc.tensor.matmul(B[2][:, :], neg_half_sum[:, :], k_sq_hi[:, :], start=False, stop=False)
                    nc.tensor.matmul(B[2][:, :], neg_half_sum[:, :], k_sq_lo[:, :], start=False, stop=True).then_inc(pe_fk, 1)
                if live(b):
                    pe.wait_ge(dv_att, b + 1)
                    for t in range(GT):
                        mm = nc.tensor.transpose(B[4][:, t * P:(t + 1) * P], attn[:, t, :], ident[:, :])
                    mm.then_inc(pe_attT, 1)
                if live(c):
                    pe.wait_ge(ac_x2T, c + 1)
                    if not first(c):
                        pe.wait_ge(dv_both, c)
                    for t in range(GT):
                        mm = nc.tensor.matmul(B[7][:, t * EXPERTS:(t + 1) * EXPERTS], x2T[:, t, :], router_s[:, :],
                                              start=True, stop=True)
                    mm.then_inc(pe_logit, 1)
                if live(b):
                    pe.wait_ge(ac_attT, b + 1)
                    nc.tensor.matmul(B[5][:, :], ones_b[:, :], bo_split[:, :, :].rearrange("p t d -> p (t d)"),
                                     start=True, stop=False)
                    for t in range(GT):
                        mm = nc.tensor.matmul(B[5][:, t * P:(t + 1) * P], attnT[:, t, :], woT_s[:, :],
                                              start=False, stop=(t == GT - 1))
                    mm.then_inc(pe_wo, 1)

            stage_a_turns(pe, turn)

            def experts_of(lo, count):
                return nc.values_load_multi_w_load_instructions(
                    blk_expert_i[0:1, bass.ds(lo + LEAD, count)], (mybir.EngineType.PE,),
                    min_val=0, max_val=EXPERTS - 1,
                    skip_runtime_bounds_check_because="the table holds a count of experts, at most the last")[1]

            def xT_blk(i, u, start):
                j = i * UNROLL + u
                pe.wait_ge(blk_loaded[u], 16 * (i + 1))
                if not start:
                    pe.wait_ge(d_xTc, j - 1)
                nc.tensor.transpose(B[4 + u % 2][:, 0:P], blk_in[:, u, 0:DIM], ident[:, :]).then_inc(d_xT, 1)

            def up(j, u, e, start):
                pe.wait_ge(d_xTc, j + 1)
                if not start:
                    pe.wait_ge(d_mul, j - 1)
                parts = [(blk_xT_hi, w13_hi), (blk_xT_hi, w13_lo), (blk_xT_lo, w13_hi)]
                for n, (rows, weights) in enumerate(parts):
                    mm = nc.tensor.matmul(B[u % 2][:, :], rows[:, u % 2, :],
                                          weights[:, bass.ds(e, 1), :].rearrange("p a i -> p (a i)"),
                                          start=(n == 0), stop=(n == 2))
                mm.then_inc(d_h, 1)

            def hidT(j, u, start):
                pe.wait_ge(d_mul, j + 1)
                if not start:
                    pe.wait_ge(d_hTc, j - 1)
                for c in range(2):
                    mm = nc.tensor.transpose(B[2 + u % 2][:, c * P:(c + 1) * P], hidden[:, u % 2, c * P:(c + 1) * P],
                                             ident[:, :])
                mm.then_inc(d_hT, 1)

            def down(j, u, e, start):
                pe.wait_ge(d_hTc, j + 1)
                if not start:
                    pe.wait_ge(d_yw, j - 1)
                for c in range(2):
                    mm = nc.tensor.matmul(B[6 + u % 2][:, 0:DIM], hiddenT[:, u % 2, c * P:(c + 1) * P],
                                          w2_s[:, bass.ds(e, 1), c, :].rearrange("p a d -> p (a d)"),
                                          start=(c == 0), stop=(c == 1))
                mm.then_inc(d_y, 1)

            def expert_turn(i, start, end):
                if start:
                    es = dict(zip(range(UNROLL), experts_of(0, UNROLL)))
                    xT_blk(0, 0, True)
                    xT_blk(0, 1, True)
                else:
                    es = dict(zip(range(-LEAD, UNROLL), experts_of(i * UNROLL - LEAD, LEAD + UNROLL)))
                for u in range(UNROLL):
                    j = i * UNROLL + u
                    up(j, u, es[u], start and u < 2)
                    if u < UNROLL - 2:
                        xT_blk(i, u + 2, False)
                    elif not end:
                        xT_blk(i + 1, u + 2 - UNROLL, False)
                    if not (start and u == 0):
                        hidT(j - 1, u + 1, start and u < 3)
                    if not (start and u < 2):
                        down(j - 2, u, es[u - 2], start and u < 4)

            pe.wait_ge(w13_l, EXPERTS)
            pe.wait_ge(w2_in, 16)
            pe.wait_ge(table_ready, 1)
            expert_turn(0, True, False)
            with pe.Fori(1, TURNS // 2) as i:
                expert_turn(i, False, False)
            pe.wait_ge(table_ready, 2)
            with pe.Fori(TURNS // 2, TURNS - 1) as i:
                expert_turn(i, False, False)
            expert_turn(TURNS - 1, False, True)
            last = TURNS * UNROLL - 1
            el = experts_of(last - 3, 4)[2:]
            hidT(last, 1, False)
            down(last - 1, 0, el[0], False)
            down(last, 1, el[1], False)


def kernel(**inputs):
    import numpy as _np
    import concourse.bacc as _bacc
    from concourse import mybir as _mybir
    from concourse.bass_utils import run_bass_kernel_spmd as _run

    get = {k: _np.asarray(v) for k, v in inputs.items()}
    wq, wk, wv, wo = (get["L0_attn_W" + c] for c in "qkvo")
    bq, bk, bv, bo = (get["L0_attn_b" + c] for c in "qkvo")
    h, e = HEADS, HEAD_DIM
    laid = {
        "x": get["L0_attn_x"],
        "weights_fold": _np.concatenate(
            [_np.broadcast_to(get["L0_attn_R"][None, :, None, :], (h, e, h, e)).reshape(P, P), wq, wk,
             bq.reshape(P, 1), bk.reshape(P, 1)], axis=1),
        "weights_rest": _np.concatenate(
            [wq.T, wk.T, wv.T, wo.T, _np.broadcast_to(bv, (P, DIM)), _np.broadcast_to(bo, (P, DIM)),
             get["L0_ffn_router_w"].T], axis=1),
        "w13": get["L0_ffn_w13"].transpose(1, 0, 2),
        "w2": get["L0_ffn_w2"].reshape(EXPERTS, 2, P, DIM).transpose(2, 0, 1, 3),
    }
    nc = _bacc.Bacc("TRN2", target_bir_lowering=False, num_devices=1)
    arrays, args = {}, []
    for name, a in laid.items():
        a = _np.ascontiguousarray(a)
        arrays[f"in_{name}"] = a
        args.append(nc.dram_tensor(f"in_{name}", a.shape, _mybir.dt.from_np(a.dtype), kind="ExternalInput").ap())
    args.append(nc.dram_tensor("out_0", (BATCHES, SEQ, DIM), _mybir.dt.float32, kind="ExternalOutput").ap())
    moe_kernel(nc, *args)
    r = _run(nc, [arrays], core_ids=[0])
    return r.results[0]["out_0"]
```
